# Optimizing a Trainium2 kernel written in Bass

```python
import numpy as np
import jax
import jax.numpy as jnp

def _softmax(x, axis=-1):
    return jax.nn.softmax(x, axis=axis)

def _gelu(x):
    return jax.nn.gelu(x, approximate=True)

def _silu(x):
    return jax.nn.silu(x)

def _sigmoid(x):
    return jax.nn.sigmoid(x)

def _layernorm(x, axis=-1, eps=1e-05):
    m = jnp.mean(x, axis=axis, keepdims=True)
    v = jnp.var(x, axis=axis, keepdims=True)
    return (x - m) / jnp.sqrt(v + eps)

def _scatter_add(tgt, idx, src, axis=0):
    return tgt.at[idx].add(src)

def _segment_sum(src, seg, n):
    return jax.ops.segment_sum(src, seg, n)
kernel_name = 'mk_vit_tower_postln_d1_tok_img1024_r4_1ee1a2'

def setup_inputs(seed: int=0):
    np.random.seed(seed)
    _w = jnp.asarray

    def _rec_inputs():
        import jax
        import jax.numpy as jnp
        _rk = jax.random.key(seed)
        x = -0.00016672 + 0.999947 * jax.random.normal(jax.random.fold_in(_rk, 1), (64, 3, 96, 96), jnp.float32)
        return x
    x = _rec_inputs()

    def _L0_tok_setup():
        import jax, jax.numpy as jnp
        import numpy as np
        PATCH = 16

        def _patchify(x, p):
            B, C, H, W = x.shape
            nh, nw = (H // p, W // p)
            x = x.reshape(B, C, nh, p, nw, p)
            x = x.transpose(0, 2, 4, 1, 3, 5)
            return x.reshape(B, nh * nw, C * p * p)
        key = jax.random.key(seed)
        k1, k2, k3, k4, k5 = jax.random.split(key, 5)
        B, C, H = (64, 3, 96)
        d_model = 256
        p = PATCH
        num_patches = (H // p) ** 2
        in_dim = p * p * C
        x = jax.random.normal(k1, (B, C, H, H), dtype=jnp.float32)
        bound = 1.0 / np.sqrt(in_dim)
        W = jax.random.uniform(k2, (d_model, in_dim), dtype=jnp.float32, minval=-bound, maxval=bound)
        b = jax.random.uniform(k3, (d_model,), dtype=jnp.float32, minval=-bound, maxval=bound)
        cls_token = jax.random.normal(k4, (1, 1, d_model), dtype=jnp.float32)
        pos_enc = jax.random.normal(k5, (1, num_patches + 1, d_model), dtype=jnp.float32)
        return {'x': x, 'W': W, 'b': b, 'cls_token': cls_token, 'pos_enc': pos_enc}
    _L0_tok_all = _L0_tok_setup()
    _L0_tok_in = {k: v for k, v in _L0_tok_all.items() if k in ('W', 'b', 'cls_token', 'pos_enc')}
    del _L0_tok_all

    def _L0_attn_setup():
        import jax, jax.numpy as jnp
        import numpy as np
        D_MODEL = 256
        D_STATE = 16
        D_CONV = 4
        EXPAND = 2
        D_INNER = D_MODEL * EXPAND
        BATCH = 2
        SEQ = 512

        def _silu(v):
            return v * jax.nn.sigmoid(v)
        key = jax.random.key(seed)
        ks = jax.random.split(key, 8)

        def rn(k, shape, scale):
            return jax.random.normal(k, shape, jnp.float32) * scale
        x = rn(ks[0], (BATCH, SEQ, D_MODEL), 1.0)
        W_in = rn(ks[1], (2 * D_INNER, D_MODEL), 0.02)
        conv_w = rn(ks[2], (D_INNER, 1, D_CONV), 0.2)
        conv_b = rn(ks[3], (D_INNER,), 0.02)
        W_x = rn(ks[4], (2 * D_STATE + 1, D_INNER), 0.02)
        W_dt = rn(ks[5], (D_INNER, 1), 0.5)
        b_dt = rn(ks[6], (D_INNER,), 0.02)
        A_log = jnp.log(jnp.broadcast_to(jnp.arange(1, D_STATE + 1, dtype=jnp.float32), (D_INNER, D_STATE)))
        D_param = jnp.ones((D_INNER,), jnp.float32)
        W_out = rn(ks[7], (D_MODEL, D_INNER), 0.02)
        return dict(x=x, W_in=W_in, conv_w=conv_w, conv_b=conv_b, W_x=W_x, W_dt=W_dt, b_dt=b_dt, A_log=A_log, D_param=D_param, W_out=W_out)
    _L0_attn_all = _L0_attn_setup()
    _L0_attn_in = {k: v for k, v in _L0_attn_all.items() if k in ('W_in', 'conv_w', 'conv_b', 'W_x', 'W_dt', 'b_dt', 'A_log', 'D_param', 'W_out')}
    del _L0_attn_all

    def _L0_ffn_setup():
        import jax, jax.numpy as jnp
        import numpy as np
        B, S, D = (4, 256, 256)
        I = 128
        E = 32
        TOP_K = 8
        N_GROUP = 8
        TOPK_GROUP = 4

        def _group_topk(scores):
            T = scores.shape[0]
            epg = E // N_GROUP
            group_scores = scores.reshape(T, N_GROUP, epg).sum(axis=-1)
            _, top_groups = jax.lax.top_k(group_scores, TOPK_GROUP)
            group_mask = jnp.zeros((T, N_GROUP), scores.dtype).at[jnp.arange(T)[:, None], top_groups].set(1.0)
            expert_mask = jnp.repeat(group_mask, epg, axis=1)
            masked_scores = scores * expert_mask
            topk_w, topk_i = jax.lax.top_k(masked_scores, TOP_K)
            return (topk_w, topk_i)

        def _reference_tuple_inner(hidden_states, gate_w, expert_gate, expert_up, expert_down, shared_gate_w, shared_up_w, shared_down_w):
            b, s, d = hidden_states.shape
            flat = hidden_states.reshape(-1, d)
            T = flat.shape[0]
            logits = flat @ gate_w.T
            scores = jax.nn.sigmoid(logits)
            topk_w, topk_i = _group_topk(scores)
            topk_w = topk_w / jnp.clip(topk_w.sum(axis=-1, keepdims=True), 1e-12)
            combine = jnp.zeros((T, E), flat.dtype).at[jnp.arange(T)[:, None], topk_i].add(topk_w)

            def body(acc, expert):
                wg, wu, wd, w = expert
                h = jax.nn.silu(flat @ wg.T) * (flat @ wu.T)
                return (acc + w[:, None] * (h @ wd.T), None)
            out, _ = jax.lax.scan(body, jnp.zeros_like(flat), (expert_gate, expert_up, expert_down, combine.T))
            shared = jax.nn.silu(flat @ shared_gate_w.T) * (flat @ shared_up_w.T) @ shared_down_w.T
            out = out + shared
            return (out.reshape(b, s, d), logits)
        key = jax.random.key(seed)
        ks = jax.random.split(key, 8)
        scale = 0.02
        return {'hidden_states': jax.random.normal(ks[0], (B, S, D), jnp.float32), 'gate_w': jax.random.normal(ks[1], (E, D), jnp.float32) * scale, 'expert_gate': jax.random.normal(ks[2], (E, I, D), jnp.float32) * scale, 'expert_up': jax.random.normal(ks[3], (E, I, D), jnp.float32) * scale, 'expert_down': jax.random.normal(ks[4], (E, D, I), jnp.float32) * scale, 'shared_gate_w': jax.random.normal(ks[5], (I, D), jnp.float32) * scale, 'shared_up_w': jax.random.normal(ks[6], (I, D), jnp.float32) * scale, 'shared_down_w': jax.random.normal(ks[7], (D, I), jnp.float32) * scale}
    _L0_ffn_all = _L0_ffn_setup()
    _L0_ffn_in = {k: v for k, v in _L0_ffn_all.items() if k in ('gate_w', 'expert_gate', 'expert_up', 'expert_down', 'shared_gate_w', 'shared_up_w', 'shared_down_w')}
    del _L0_ffn_all
    return {'x': x, 'L0_tok_W': _L0_tok_in['W'], 'L0_tok_b': _L0_tok_in['b'], 'L0_tok_cls_token': _L0_tok_in['cls_token'], 'L0_tok_pos_enc': _L0_tok_in['pos_enc'], 'L0_attn_W_in': _L0_attn_in['W_in'], 'L0_attn_conv_w': _L0_attn_in['conv_w'], 'L0_attn_conv_b': _L0_attn_in['conv_b'], 'L0_attn_W_x': _L0_attn_in['W_x'], 'L0_attn_W_dt': _L0_attn_in['W_dt'], 'L0_attn_b_dt': _L0_attn_in['b_dt'], 'L0_attn_A_log': _L0_attn_in['A_log'], 'L0_attn_D_param': _L0_attn_in['D_param'], 'L0_attn_W_out': _L0_attn_in['W_out'], 'L0_ffn_gate_w': _L0_ffn_in['gate_w'], 'L0_ffn_expert_gate': _L0_ffn_in['expert_gate'], 'L0_ffn_expert_up': _L0_ffn_in['expert_up'], 'L0_ffn_expert_down': _L0_ffn_in['expert_down'], 'L0_ffn_shared_gate_w': _L0_ffn_in['shared_gate_w'], 'L0_ffn_shared_up_w': _L0_ffn_in['shared_up_w'], 'L0_ffn_shared_down_w': _L0_ffn_in['shared_down_w']}

def reference(x, L0_tok_W, L0_tok_b, L0_tok_cls_token, L0_tok_pos_enc, L0_attn_W_in, L0_attn_conv_w, L0_attn_conv_b, L0_attn_W_x, L0_attn_W_dt, L0_attn_b_dt, L0_attn_A_log, L0_attn_D_param, L0_attn_W_out, L0_ffn_gate_w, L0_ffn_expert_gate, L0_ffn_expert_up, L0_ffn_expert_down, L0_ffn_shared_gate_w, L0_ffn_shared_up_w, L0_ffn_shared_down_w):
    import jax
    import jax.numpy as jnp

    def _L0_tok_ref(x, W, b, cls_token, pos_enc):
        import jax, jax.numpy as jnp
        import numpy as np
        PATCH = 16

        def _patchify(x, p):
            B, C, H, W = x.shape
            nh, nw = (H // p, W // p)
            x = x.reshape(B, C, nh, p, nw, p)
            x = x.transpose(0, 2, 4, 1, 3, 5)
            return x.reshape(B, nh * nw, C * p * p)
        B = x.shape[0]
        patches = _patchify(x, PATCH)
        proj = jnp.einsum('bnf,df->bnd', patches, W) + b
        cls = jnp.broadcast_to(cls_token, (B, 1, cls_token.shape[-1]))
        out = jnp.concatenate([cls, proj], axis=1) + pos_enc
        return out

    def _L0_attn_ref(x, W_in, conv_w, conv_b, W_x, W_dt, b_dt, A_log, D_param, W_out):
        import jax, jax.numpy as jnp
        import numpy as np
        D_MODEL = 256
        D_STATE = 16
        D_CONV = 4
        EXPAND = 2
        D_INNER = D_MODEL * EXPAND
        BATCH = 2
        SEQ = 512

        def _silu(v):
            return v * jax.nn.sigmoid(v)
        B, T, _ = x.shape
        xz = jnp.einsum('btm,im->bti', x, W_in)
        x_d, z = jnp.split(xz, 2, axis=-1)
        xc = jnp.moveaxis(x_d, 1, 2)
        xc = jnp.pad(xc, ((0, 0), (0, 0), (D_CONV - 1, 0)))
        xc = jax.lax.conv_general_dilated(xc, conv_w, window_strides=(1,), padding='VALID', feature_group_count=D_INNER, dimension_numbers=('NCH', 'OIH', 'NCH'))
        x_d = _silu(jnp.moveaxis(xc + conv_b[None, :, None], 1, 2))
        A = -jnp.exp(A_log)
        ssm_in = jnp.einsum('btd,kd->btk', x_d, W_x)
        dt_raw = ssm_in[..., :1]
        B_mat = ssm_in[..., 1:1 + D_STATE]
        C_mat = ssm_in[..., 1 + D_STATE:]
        delta = jax.nn.softplus(dt_raw * W_dt[:, 0] + b_dt)

        def step(h, inp):
            d_t, b_t, c_t, u_t = inp
            dA = jnp.exp(d_t[..., None] * A)
            h = dA * h + d_t[..., None] * b_t[:, None, :] * u_t[..., None]
            y = jnp.einsum('bds,bs->bd', h, c_t)
            return (h, y)
        h0 = jnp.zeros((B, D_INNER, D_STATE), x.dtype)
        xs = (jnp.moveaxis(delta, 1, 0), jnp.moveaxis(B_mat, 1, 0), jnp.moveaxis(C_mat, 1, 0), jnp.moveaxis(x_d, 1, 0))
        _, ys = jax.lax.scan(step, h0, xs)
        y = jnp.moveaxis(ys, 0, 1) + D_param * x_d
        y = y * _silu(z)
        return jnp.einsum('btd,md->btm', y, W_out)

    def _L0_ffn_ref(hidden_states, gate_w, expert_gate, expert_up, expert_down, shared_gate_w, shared_up_w, shared_down_w):
        import jax, jax.numpy as jnp
        import numpy as np
        B, S, D = (4, 256, 256)
        I = 128
        E = 32
        TOP_K = 8
        N_GROUP = 8
        TOPK_GROUP = 4

        def _group_topk(scores):
            T = scores.shape[0]
            epg = E // N_GROUP
            group_scores = scores.reshape(T, N_GROUP, epg).sum(axis=-1)
            _, top_groups = jax.lax.top_k(group_scores, TOPK_GROUP)
            group_mask = jnp.zeros((T, N_GROUP), scores.dtype).at[jnp.arange(T)[:, None], top_groups].set(1.0)
            expert_mask = jnp.repeat(group_mask, epg, axis=1)
            masked_scores = scores * expert_mask
            topk_w, topk_i = jax.lax.top_k(masked_scores, TOP_K)
            return (topk_w, topk_i)

        def _reference_tuple_inner(hidden_states, gate_w, expert_gate, expert_up, expert_down, shared_gate_w, shared_up_w, shared_down_w):
            b, s, d = hidden_states.shape
            flat = hidden_states.reshape(-1, d)
            T = flat.shape[0]
            logits = flat @ gate_w.T
            scores = jax.nn.sigmoid(logits)
            topk_w, topk_i = _group_topk(scores)
            topk_w = topk_w / jnp.clip(topk_w.sum(axis=-1, keepdims=True), 1e-12)
            combine = jnp.zeros((T, E), flat.dtype).at[jnp.arange(T)[:, None], topk_i].add(topk_w)

            def body(acc, expert):
                wg, wu, wd, w = expert
                h = jax.nn.silu(flat @ wg.T) * (flat @ wu.T)
                return (acc + w[:, None] * (h @ wd.T), None)
            out, _ = jax.lax.scan(body, jnp.zeros_like(flat), (expert_gate, expert_up, expert_down, combine.T))
            shared = jax.nn.silu(flat @ shared_gate_w.T) * (flat @ shared_up_w.T) @ shared_down_w.T
            out = out + shared
            return (out.reshape(b, s, d), logits)
        return _reference_tuple_inner(hidden_states, gate_w, expert_gate, expert_up, expert_down, shared_gate_w, shared_up_w, shared_down_w)[0]
    h = _L0_tok_ref(x, L0_tok_W, L0_tok_b, L0_tok_cls_token, L0_tok_pos_enc)
    h = _layernorm(h + _L0_attn_ref(h, L0_attn_W_in, L0_attn_conv_w, L0_attn_conv_b, L0_attn_W_x, L0_attn_W_dt, L0_attn_b_dt, L0_attn_A_log, L0_attn_D_param, L0_attn_W_out), axis=-1)
    h = _layernorm(h + _L0_ffn_ref(h, L0_ffn_gate_w, L0_ffn_expert_gate, L0_ffn_expert_up, L0_ffn_expert_down, L0_ffn_shared_gate_w, L0_ffn_shared_up_w, L0_ffn_shared_down_w), axis=-1)
    return h

_drawn_inputs = setup_inputs


def setup_inputs(seed=0):
    import zlib

    import numpy as np

    out = dict(_drawn_inputs(seed))
    spreads = {'L0_attn_D_param': (1.0, 0.6)}
    factors = {'L0_tok_b': 3.037,
     'L0_attn_W_in': 8.0,
     'L0_attn_conv_w': 8.0,
     'L0_attn_conv_b': 8.0,
     'L0_attn_W_x': 8.0,
     'L0_attn_W_dt': 8.0,
     'L0_attn_b_dt': 8.0,
     'L0_attn_A_log': 8.0,
     'L0_attn_W_out': 8.0,
     'L0_ffn_gate_w': 8.0,
     'L0_ffn_expert_gate': 8.0,
     'L0_ffn_expert_up': 8.0,
     'L0_ffn_expert_down': 8.0,
     'L0_ffn_shared_gate_w': 4.898,
     'L0_ffn_shared_up_w': 4.819,
     'L0_ffn_shared_down_w': 4.834}
    for name, (base, spread) in spreads.items():
        noise = np.random.default_rng([zlib.crc32(name.encode()), seed]).standard_normal(out[name].shape)
        drawn = base * np.exp(spread * noise) if base else spread * noise
        out[name] = jnp.asarray(drawn.astype(out[name].dtype))
    for name, factor in factors.items():
        out[name] = (out[name] * factor).astype(out[name].dtype)
    return out
```

```python
from contextlib import ExitStack

import concourse.bass as bass
from concourse import mybir

F32 = mybir.dt.float32
BF16 = mybir.dt.bfloat16
ALU = mybir.AluOpType
ACT = mybir.ActivationFunctionType
AX = mybir.AxisListType

P = 128
IMAGES, CHANNELS, SIDE, PATCH = 64, 3, 96, 16
GRID = SIDE // PATCH
PATCHES = GRID * GRID
TOKENS = PATCHES + 1
FEATS = CHANNELS * PATCH * PATCH
DM, DI, STATES, TAPS = 256, 512, 16, 4
EXPERTS, TOPK, GROUPS, TOPG, HID = 32, 8, 8, 4, 128
PER_GROUP = EXPERTS // GROUPS
TI = 6
TILES = -(-IMAGES // TI)
N = TI * TOKENS
NB = N // 2
NP = TI * PATCHES
KF, KM, KI = FEATS // P, DM // P, DI // P
PADT = TOKENS + TAPS - 1
ROWS = 2 * STATES
SPLIT = 3 * ROWS
WCOLS = 4 * P + DM
SLOTS = 4
PAIRS = STATES // 2
EPS = 1e-5
SMALL = 2.0 ** -11


def build(nc, x, w_tok, b_tok, cls_tok, pos, w_in, conv_w, conv_b, w_x, w_dt, b_dt, a_log, d_par, w_out,
          gate_w, experts, shared, out):
    with ExitStack() as ctx:
        def sb(name, shape, dt=F32):
            return ctx.enter_context(nc.sbuf_tensor(name, shape, dt))

        def ps(name):
            return ctx.enter_context(nc.psum_tensor(name, [P, 512], F32))

        def sem(name):
            return ctx.enter_context(nc.semaphore(name))

        tokw = sb("tokw", [P, KF, DM])
        inw = sb("inw", [P, KM, 2 * DI])
        outw = sb("outw", [P, KI, DM])
        gatew = sb("gatew", [P, KM, EXPERTS])
        sharedw = sb("sharedw", [P, WCOLS])
        xw_raw = sb("xw_raw", [P, KI, 1 + ROWS])
        xw = sb("xw", [P, KI, 3, ROWS])
        dtw = sb("dtw", [P, KI, P])
        posb = sb("posb", [P, KM, TOKENS])
        tokb = sb("tokb", [P, KM])
        clsb = sb("clsb", [P, KM])
        convw = sb("convw", [P, KI, TAPS])
        convb = sb("convb", [P, KI])
        dt_scale = sb("dt_scale", [P, KI])
        dt_bias = sb("dt_bias", [P, KI])
        alog = sb("alog", [P, KI * STATES])
        aexp = sb("aexp", [P, KI * STATES])
        aneg = sb("aneg", [P, STATES, KI])
        dpar = sb("dpar", [P, KI])
        ident = sb("ident", [P, P])
        diag_d = sb("diag_d", [P, KI, P])
        averager = sb("averager", [P, P])
        sel = sb("sel", [SPLIT, ROWS, P], BF16)
        one_col = sb("one_col", [P, 1])
        eps_col = sb("eps_col", [P, 1])
        small_col = sb("small_col", [P, 1])
        ln_small = sb("ln_small", [P, 1])

        patches = sb("patches", [P, KF, NP])
        h0 = sb("h0", [P, KM, N])
        xpad = sb("xpad", [P, KI, TI, PADT])
        conv = sb("conv", [P, KI, N])
        half_tanh = sb("half_tanh", [P, KI, N])
        half_tanh_z = sb("half_tanh_z", [P, KI, N])
        x2 = sb("x2", [P, KI, N])
        z2 = sb("z2", [P, KI, N])
        delta = sb("delta", [P, KI, N])
        soft = sb("soft", [P, KI, N])
        small = sb("small", [P, KI, N])
        series = sb("series", [P, KI, N])
        du = sb("du", [P, KI, N])
        bc_rows = sb("bc_rows", [SPLIT, N], BF16)
        w_rows = sb("w_rows", [SPLIT, N], BF16)
        rest = sb("rest", [SPLIT, N])
        mid = sb("mid", [SPLIT, N], BF16)
        decay = [sb(f"decay{q}", [P, KI * TI, TOKENS]) for q in range(2)]
        drive = [sb(f"drive{q}", [P, KI, N]) for q in range(2)]
        state = [sb(f"state{q}", [P, KI, N]) for q in range(2)]
        read = [sb(f"read{q}", [P, KI, N]) for q in range(2)]
        gated = sb("gated", [P, KI, N])
        r1 = sb("r1", [P, KM, N])
        r2 = sb("r2", [P, KM, N])
        centred = sb("centred", [P, KM, N])
        squared = sb("squared", [P, KM, N])
        rough = sb("rough", [P, N])
        newton = sb("newton", [P, 2, N])
        rstd = sb("rstd", [P, N])
        h1 = sb("h1", [P, KM, N])
        outb = sb("outb", [P, KM, N])

        ex = sb("ex", [NB, 2, EXPERTS])
        score = sb("score", [NB, 2, EXPERTS])
        gsum = sb("gsum", [NB, 2, GROUPS + 8 - TOPG])
        gtop = sb("gtop", [NB, 2, 8])
        glist = sb("glist", [NB, 2, 8])
        gleft = sb("gleft", [NB, 2, GROUPS + 8 - TOPG])
        gmask = sb("gmask", [NB, 2, GROUPS])
        masked = sb("masked", [NB, 2, EXPERTS])
        etop = sb("etop", [NB, 2, 8])
        eleft = sb("eleft", [NB, 2, EXPERTS])
        wsel = sb("wsel", [NB, 2, EXPERTS])
        wsum = sb("wsum", [NB, 2])
        winv = sb("winv", [NB, 2])
        w3 = sb("w3", [NB, 2, 3, EXPERTS])

        expw = [sb(f"expw{k}", [P, WCOLS]) for k in range(SLOTS)]
        tanh_g = sb("tanh_g", [P, 2, N])
        act_g = sb("act_g", [P, 2, N])
        hid = sb("hid", [P, 2, N])
        hidw = [sb(f"hidw{q}", [P, 2, N]) for q in range(2)]
        tanh_s = sb("tanh_s", [P, N])
        act_s = sb("act_s", [P, N])
        hid_s = sb("hid_s", [P, N])

        Y = [ps("Y0"), ps("Y1")]
        GUt = ctx.enter_context(nc.psum_tensor("GU", [P, 2, 512], F32))
        GU = [GUt[:, 0, :], GUt[:, 1, :]]
        BC = [ps("BC0"), ps("BC1")]
        O = ps("O")
        W = ps("W")

        def two(bank):
            return bank[:, 0:2 * N].rearrange("p (c n) -> p c n", c=2)

        weights_in = sem("weights_in")
        consts_pool = sem("consts_pool")
        aexp_done = sem("aexp_done")
        consts_dve = sem("consts_dve")
        setup_done = sem("setup_done")
        patches_in = sem("patches_in")
        tok_done = sem("tok_done")
        h0_done = sem("h0_done")
        xz_done = sem("xz_done")
        xpad_done = sem("xpad_done")
        tap_done = sem("tap_done")
        conv_done = sem("conv_done")
        conv_tanh = sem("conv_tanh")
        z_tanh = sem("z_tanh")
        x2_done = sem("x2_done")
        z2_done = sem("z2_done")
        dt_done = sem("dt_done")
        rows_done = sem("rows_done")
        split_step = sem("split_step")
        soft_step = sem("soft_step")
        small_done = sem("small_done")
        series_done = sem("series_done")
        softplus_step = sem("softplus_step")
        delta_done = sem("delta_done")
        du_done = sem("du_done")
        y_init = sem("y_init")
        bc_done = sem("bc_done")
        decay_done = sem("decay_done")
        drive_done = sem("drive_done")
        decay_free = sem("decay_free")
        bc_free = sem("bc_free")
        read_free = sem("read_free")
        gated_done = sem("gated_done")
        outproj_done = sem("outproj_done")
        r_done = sem("r_done")
        mean_done = sem("mean_done")
        centred_done = sem("centred_done")
        squared_done = sem("squared_done")
        var_done = sem("var_done")
        rough_step = sem("rough_step")
        newton_step = sem("newton_step")
        norm_done = sem("norm_done")
        logits_done = sem("logits_done")
        ex_done = sem("ex_done")
        route_step = sem("route_step")
        route_gate = sem("route_gate")
        w3_turned = sem("w3_turned")
        shared_gu = sem("shared_gu")
        shared_tanh = sem("shared_tanh")
        shared_step = sem("shared_step")
        shared_down = sem("shared_down")
        expert_in = [sem(f"expert_in{k}") for k in range(SLOTS)]
        gu_done = sem("gu_done")
        tanh_done = sem("tanh_done")
        act_done = sem("act_done")
        gu_free = sem("gu_free")
        wb_done = sem("wb_done")
        wb_free = sem("wb_free")
        hidw_free = sem("hidw_free")
        out_sent = sem("out_sent")

        LOADS = [(tokw, w_tok), (inw, w_in), (outw, w_out), (gatew, gate_w), (sharedw, shared), (xw_raw, w_x),
                 (posb, pos), (tokb, b_tok), (clsb, cls_tok), (convw, conv_w), (convb, conv_b),
                 (dt_scale, w_dt), (dt_bias, b_dt), (alog, a_log), (dpar, d_par)]
        CONSTS_POOL = 3
        CONV_OPS = KI * (TAPS - 1)
        SPLITS = 4
        ROUTE = 19
        LNS = 2

        def tiles(eng, tile):
            tile(0, True, False)
            with eng.Fori(1, TILES) as i:
                tile(i, True, True)
            tile(TILES, False, True)

        def norm_no(i, which):
            return 2 * i if which == 0 else 2 * i - 1

        block = ctx.enter_context(nc.Block())

        @block.sync
        def _(sp):
            sp.sem_inc(out_sent, 16)
            for to, of in LOADS:
                sp.dma_start(to[:], of).then_inc(weights_in, 16)
            sp.dma_start(patches[:], x[0]).then_inc(patches_in, 16)

            def expert_pair(t, p):
                for k in range(SLOTS):
                    sp.wait_ge(hidw_free, 2 * (PAIRS * t + p) + k // 2 + 1)
                    sp.dma_start(expw[k][:], experts[SLOTS * p + k]).then_inc(expert_in[k], 16)

            def tile(t, more):
                if more:
                    sp.wait_ge(tok_done, t + 1)
                    sp.dma_start(patches[:], x[t + 1]).then_inc(patches_in, 16)
                with sp.Fori(0, PAIRS) as p:
                    expert_pair(t, p)
                sp.wait_ge(norm_done, 2 * t + 2)
                sp.dma_start(out[t], outb[:]).then_inc(out_sent, 16)

            with sp.Fori(0, TILES - 1) as t:
                tile(t, True)
            tile(TILES - 1, False)
            sp.wait_ge(out_sent, 16 * (TILES + 1))

        @block.gpsimd
        def _(pool):
            nc.gpsimd.memset(ident[:], 0.0).then_inc(consts_pool, 1)
            nc.gpsimd.memset(sel[:], 0.0).then_inc(consts_pool, 1)
            pool.wait_ge(consts_pool, 2)
            nc.gpsimd.affine_select(out=ident[:], in_=ident[:], compare_op=ALU.not_equal, fill=1.0, base=0,
                                    pattern=[[-1, P]], channel_multiplier=1).then_inc(consts_pool, 1)
            for part in range(3):
                nc.gpsimd.affine_select(out=sel[:], in_=sel[:], compare_op=ALU.not_equal, fill=1.0,
                                        base=-ROWS * part, pattern=[[-1, ROWS], [0, P]],
                                        channel_multiplier=1).then_inc(consts_pool, 1)
                pool.wait_ge(consts_pool, 4 + part)
            nc.gpsimd.memset(xpad[:], 0.0).then_inc(consts_pool, 1)
            for q in range(2):
                nc.gpsimd.memset(decay[q][:], 0.0).then_inc(consts_pool, 1)
            nc.gpsimd.memset(glist[:], -2.0).then_inc(consts_pool, 1)
            nc.gpsimd.memset(gsum[:], -2.0).then_inc(consts_pool, 1)

        CONSTS_POOL = 11

        @block.tensor
        def _(pe):
            pe.sem_inc(read_free, 2)
            pe.sem_inc(hidw_free, 2)
            pe.wait_ge(weights_in, 16 * len(LOADS))
            pe.wait_ge(consts_pool, CONSTS_POOL)
            pe.wait_ge(setup_done, 1)

            def prologue(i):
                pe.wait_ge(patches_in, 16 * (i + 1))
                for m in range(KM):
                    for k in range(KF):
                        mm = nc.tensor.matmul(GU[0][:, m * NP:(m + 1) * NP], tokw[:, k, m * P:(m + 1) * P],
                                              patches[:, k, :], start=(k == 0), stop=(k == KF - 1))
                mm.then_inc(tok_done, 1)
                pe.wait_ge(h0_done, i + 1)
                for c in range(2 * KI):
                    bank = (Y + BC)[c // 2]
                    for k in range(KM):
                        mm = nc.tensor.matmul(bank[:, (c % 2) * N:(c % 2 + 1) * N], inw[:, k, c * P:(c + 1) * P],
                                              h0[:, k, :], start=(k == 0), stop=(k == KM - 1))
                    if c % 2:
                        mm.then_inc(xz_done, 1)
                pe.wait_ge(x2_done, i + 1)
                for c in range(KI):
                    mm = nc.tensor.matmul(GU[1][:, 0:N], dtw[:, c, :], x2[:, c, :], start=(c == 0), stop=(c == KI - 1))
                mm.then_inc(dt_done, 1)
                for c in range(KI):
                    mm = nc.tensor.matmul(W[0:SPLIT, 0:N], xw[:, c].rearrange("p a b -> p (a b)"), x2[:, c, :],
                                          start=(c == 0), stop=(c == KI - 1))
                mm.then_inc(rows_done, 1)
                for c in range(KI):
                    mm = nc.tensor.matmul(Y[c // 2][:, (c % 2) * N:(c % 2 + 1) * N], diag_d[:, c, :], x2[:, c, :],
                                          start=(c % 2 == 0), stop=False, skip_group_check=True)
                pe.wait_ge(split_step, SPLITS * 2 * i + SPLITS)
                pe.wait_ge(z2_done, 2 * i + 2)

            def shared_expert(i, mamba):
                if mamba:
                    pe.wait_ge(soft_step, 3 * i + 1)
                for g in range(2):
                    for k in range(KM):
                        mm = nc.tensor.matmul(GU[1][:, g * N:(g + 1) * N], sharedw[:, (2 * g + k) * P:(2 * g + k + 1) * P],
                                              h1[:, k, :], start=(k == 0), stop=(k == KM - 1))
                mm.then_inc(shared_gu, 1)
                pe.wait_ge(shared_step, 2 * (i - 1) + 2)
                for m in range(KM):
                    mm = nc.tensor.matmul(O[:, m * N:(m + 1) * N], sharedw[:, (4 + m) * P:(5 + m) * P], hid_s[:],
                                          start=(m == 0), stop=False, skip_group_check=True)
                pe.wait_ge(split_step, SPLITS * 2 * i)

            def spread_bc(i, s, q):
                pe.wait_ge(bc_free, STATES * i + s + 1)
                for j in range(2):
                    mm = nc.tensor.matmul(BC[q][:, j * N:(j + 1) * N], sel[:, STATES * j + s, :], bc_rows[:],
                                          start=True, stop=True)
                mm.then_inc(bc_done, 1)

            def gate_up(i, p, s, q):
                pe.wait_ge(gu_free, STATES * (i - 1) + s + 1)
                for j in range(2):
                    pe.wait_ge(expert_in[2 * q + j], 16 * (PAIRS * (i - 1) + p + 1))
                    for g in range(2):
                        for k in range(KM):
                            mm = nc.tensor.matmul(GU[g][:, j * N:(j + 1) * N],
                                                  expw[2 * q + j][:, (2 * g + k) * P:(2 * g + k + 1) * P],
                                                  h1[:, k, :], start=(k == 0), stop=(k == KM - 1))
                mm.then_inc(gu_done, 1)
                pe.wait_ge(wb_free, STATES * (i - 1) + s + 1)
                for j in range(2):
                    mm = nc.tensor.matmul(W[:, j * N:(j + 1) * N], sel[:, 2 * s + j, :], w_rows[:], start=True, stop=True)
                mm.then_inc(wb_done, 1)

            def sum_y(i, s, q):
                pe.wait_ge(bc_free, STATES * i + s + 3)
                for b in range(2):
                    mm = nc.tensor.matmul(Y[b][:, 0:2 * N], ident[:], read[q][:, 2 * b:2 * b + 2, :].rearrange("p c n -> p (c n)"),
                                          start=False, stop=False, skip_group_check=True)
                mm.then_inc(read_free, 1)

            def down(i, s, q):
                pe.wait_ge(wb_free, STATES * (i - 1) + s + 2)
                for j in range(2):
                    for m in range(KM):
                        mm = nc.tensor.matmul(O[:, m * N:(m + 1) * N], expw[2 * q + j][:, (4 + m) * P:(5 + m) * P],
                                              hidw[q][:, j, :], start=False, stop=False, skip_group_check=True)
                mm.then_inc(hidw_free, 1)

            def norm(no, source):
                pe.wait_ge(r_done, no + 1)
                for k in range(KM):
                    mm = nc.tensor.matmul(GU[1][:, 0:N], averager[:], source[:, k, :], start=(k == 0), stop=(k == KM - 1))
                mm.then_inc(mean_done, 1)
                pe.wait_ge(squared_done, no + 1)
                for k in range(KM):
                    mm = nc.tensor.matmul(W[:, 0:N], averager[:], squared[:, k, :], start=(k == 0), stop=(k == KM - 1))
                mm.then_inc(var_done, 1)

            def tile(i, mamba, moe):
                if mamba:
                    prologue(i)
                if moe:
                    shared_expert(i, mamba)

                def first(p, s, q):
                    if mamba:
                        spread_bc(i, s, q)
                    if moe:
                        gate_up(i, p, s, q)

                def second(s, q):
                    if mamba:
                        sum_y(i, s, q)
                    if moe:
                        down(i, s, q)

                first(0, 0, 0)
                with pe.Fori(0, PAIRS - 1) as p:
                    first(p, 2 * p + 1, 1)
                    second(2 * p, 0)
                    first(p + 1, 2 * p + 2, 0)
                    second(2 * p + 1, 1)
                first(PAIRS - 1, STATES - 1, 1)
                second(STATES - 2, 0)
                second(STATES - 1, 1)

                if moe:
                    norm(norm_no(i, 1), r2)
                if mamba:
                    pe.wait_ge(gated_done, 2 * i + 2)
                    for m in range(KM):
                        for c in range(KI):
                            mm = nc.tensor.matmul(GU[0][:, m * N:(m + 1) * N], outw[:, c, m * P:(m + 1) * P],
                                                  gated[:, c, :], start=(c == 0), stop=(c == KI - 1))
                    mm.then_inc(outproj_done, 1)
                    norm(norm_no(i, 0), r1)
                    pe.wait_ge(norm_done, norm_no(i, 0) + 1)
                    for b in range(2):
                        for k in range(KM):
                            mm = nc.tensor.matmul(BC[1][0:NB, b * EXPERTS:(b + 1) * EXPERTS], h1[:, k, b * NB:(b + 1) * NB],
                                                  gatew[:, k, :], start=(k == 0), stop=(k == KM - 1))
                    mm.then_inc(logits_done, 1)
                    pe.wait_ge(route_step, ROUTE * (i + 1))
                    for b in range(2):
                        mm = nc.tensor.transpose(BC[0][0:SPLIT, b * NB:(b + 1) * NB],
                                                 w3[:, b].rearrange("p a e -> p (a e)"), ident[0:NB, 0:NB])
                    mm.then_inc(w3_turned, 1)

            tiles(pe, tile)

        @block.scalar
        def _(act):
            act.wait_ge(weights_in, 16 * len(LOADS))
            nc.scalar.activation(aexp[:], alog[:], ACT.Exp).then_inc(aexp_done, 1)
            act.wait_ge(consts_dve, 1)
            nc.scalar.activation(ln_small[:], small_col[:], ACT.Ln, bias=one_col[:]).then_inc(aexp_done, 1)
            act.wait_ge(consts_pool, CONSTS_POOL)
            act.wait_ge(setup_done, 1)

            def prologue(i):
                for b in range(2):
                    act.wait_ge(xz_done, 4 * i + b + 1)
                    for c in range(2 * b, 2 * b + 2):
                        src = Y[b][:, (c % 2) * N:(c % 2 + 1) * N]
                        nc.scalar.activation(xpad[:, c, :, TAPS - 1:PADT], src.rearrange("p (a t) -> p a t", a=TI),
                                             ACT.Copy).then_inc(xpad_done, 1)
                        nc.scalar.activation(conv[:, c, :], src, ACT.Identity, scale=convw[:, c, TAPS - 1:TAPS],
                                             bias=convb[:, c:c + 1]).then_inc(tap_done, 1)
                for b in range(2):
                    act.wait_ge(xz_done, 4 * i + 3 + b)
                    nc.scalar.activation(half_tanh_z[:, 2 * b:2 * b + 2, :], two(BC[b]), ACT.Tanh,
                                         scale=0.5).then_inc(z_tanh, 1)
                act.wait_ge(conv_done, CONV_OPS * (i + 1))
                nc.scalar.activation(half_tanh[:], conv[:], ACT.Tanh, scale=0.5).then_inc(conv_tanh, 1)
                act.wait_ge(dt_done, i + 1)
                for c in range(KI):
                    nc.scalar.activation(soft[:, c, :], GU[1][:, 0:N], ACT.Abs, scale=dt_scale[:, c:c + 1],
                                         bias=dt_bias[:, c:c + 1])
                    last = nc.scalar.activation(delta[:, c, :], GU[1][:, 0:N], ACT.Relu, scale=dt_scale[:, c:c + 1],
                                                bias=dt_bias[:, c:c + 1])
                last.then_inc(soft_step, 1)
                act.wait_ge(soft_step, 3 * i + 1)
                nc.scalar.activation(soft[:], soft[:], ACT.Exp, scale=-1.0).then_inc(soft_step, 1)
                act.wait_ge(soft_step, 3 * i + 2)
                act.wait_ge(small_done, i + 1)
                nc.scalar.activation(series[:], small[:], ACT.Identity, scale=-0.5, bias=one_col[:]).then_inc(series_done, 1)
                nc.scalar.activation(soft[:], soft[:], ACT.Ln, bias=one_col[:]).then_inc(soft_step, 1)
                act.wait_ge(delta_done, i + 1)

            def shared_expert(i):
                act.wait_ge(shared_gu, i)
                nc.scalar.activation(tanh_s[:], GU[1][:, 0:N], ACT.Tanh, scale=0.5).then_inc(shared_tanh, 1)

            def decays(i, s, q):
                act.wait_ge(decay_free, STATES * i + s + 1)
                for c in range(KI):
                    last = nc.scalar.activation(
                        decay[q][:, c * TI:(c + 1) * TI, 1:TOKENS],
                        delta[:, c, :].rearrange("p (a t) -> p a t", a=TI)[:, :, 1:TOKENS],
                        ACT.Exp, scale=aneg[:, s, c:c + 1])
                last.then_inc(decay_done, 1)

            def tanhs(i, s):
                act.wait_ge(gu_done, STATES * (i - 1) + s + 1)
                nc.scalar.activation(tanh_g[:], two(GU[0]), ACT.Tanh, scale=0.5).then_inc(tanh_done, 1)

            def norm(no):
                act.wait_ge(centred_done, no + 1)
                nc.scalar.activation(squared[:], centred[:], ACT.Square).then_inc(squared_done, 1)
                act.wait_ge(var_done, no + 1)
                nc.scalar.activation(rough[:], W[:, 0:N], ACT.Ln, bias=eps_col[:]).then_inc(rough_step, 1)
                act.wait_ge(rough_step, 2 * no + 1)
                nc.scalar.activation(rough[:], rough[:], ACT.Exp, scale=-0.5).then_inc(rough_step, 1)

            def tile(i, mamba, moe):
                if mamba:
                    prologue(i)
                if moe:
                    shared_expert(i)
                with act.Fori(0, PAIRS) as p:
                    for q in range(2):
                        if mamba:
                            decays(i, 2 * p + q, q)
                        if moe:
                            tanhs(i, 2 * p + q)
                if moe:
                    norm(norm_no(i, 1))
                if mamba:
                    norm(norm_no(i, 0))
                    act.wait_ge(logits_done, i + 1)
                    nc.scalar.activation(ex[:], BC[1][0:NB, 0:2 * EXPERTS].rearrange("p (b e) -> p b e", b=2), ACT.Exp,
                                         scale=-1.0).then_inc(ex_done, 1)

            tiles(act, tile)

        @block.vector
        def _(dve):
            dve.sem_inc(decay_free, 2)
            dve.sem_inc(bc_free, 2)
            dve.sem_inc(gu_free, 1)
            dve.sem_inc(wb_free, 1)

            def setup():
                made = [0]

                def made_in_turn(ins):
                    made[0] += 1
                    ins.then_inc(consts_dve, 1)
                    dve.wait_ge(consts_dve, made[0])

                nc.vector.memset(one_col[:], 1.0)
                nc.vector.memset(eps_col[:], EPS)
                nc.vector.memset(small_col[:], SMALL)
                made_in_turn(nc.vector.memset(averager[:], 1.0 / DM))
                dve.wait_ge(weights_in, 16 * len(LOADS))
                for part in range(3):
                    nc.vector.tensor_scalar(xw[:, :, part, :], xw_raw[:, :, 1:1 + ROWS], 0.5, None, ALU.mult)
                nc.vector.tensor_scalar(dtw[:], xw_raw[:, :, 0:1].broadcast_to([P, KI, P]), 0.5, None, ALU.mult)
                for m in range(KM):
                    nc.vector.tensor_scalar(posb[:, m, 0:1], posb[:, m, 0:1], clsb[:, m:m + 1], None, ALU.add)
                    nc.vector.tensor_scalar(posb[:, m, 1:TOKENS], posb[:, m, 1:TOKENS], tokb[:, m:m + 1], None, ALU.add)
                dve.wait_ge(aexp_done, 2)
                nc.vector.tensor_scalar(aneg[:].rearrange("p s c -> p c s"), aexp[:].rearrange("p (c s) -> p c s", c=KI),
                                        -1.0, None, ALU.mult)
                dve.wait_ge(consts_pool, CONSTS_POOL)
                for c in range(KI):
                    made_in_turn(nc.vector.tensor_scalar(diag_d[:, c, :], ident[:], dpar[:, c:c + 1], 0.5, ALU.mult, ALU.mult))
                nc.vector.tensor_scalar(rstd[:, 0:1], one_col[:], 1.0, None, ALU.mult).then_inc(setup_done, 1)

            setup()

            def split(no, bank, rows):
                base = SPLITS * no
                nc.vector.tensor_copy(rows[:], bank[0:SPLIT, 0:N]).then_inc(split_step, 1)
                dve.wait_ge(split_step, base + 1)
                nc.vector.tensor_tensor(rest[:], bank[0:SPLIT, 0:N], rows[:], ALU.subtract).then_inc(split_step, 1)
                dve.wait_ge(split_step, base + 2)
                nc.vector.tensor_copy(mid[:], rest[:]).then_inc(split_step, 1)
                dve.wait_ge(split_step, base + 3)
                nc.vector.tensor_copy(rows[ROWS:2 * ROWS, :], mid[ROWS:2 * ROWS, :])
                nc.vector.tensor_tensor(rows[2 * ROWS:SPLIT, :], rest[2 * ROWS:SPLIT, :], mid[2 * ROWS:SPLIT, :],
                                        ALU.subtract).then_inc(split_step, 1)

            def prologue(i):
                dve.wait_ge(tok_done, i + 1)
                for m in range(KM):
                    h0m = h0[:, m, :].rearrange("p (a t) -> p a t", a=TI)
                    nc.vector.tensor_tensor(
                        h0m[:, :, 1:TOKENS], GU[0][:, m * NP:(m + 1) * NP].rearrange("p (a t) -> p a t", a=TI),
                        posb[:, m:m + 1, 1:TOKENS].broadcast_to([P, TI, PATCHES]), ALU.add)
                    last = nc.vector.tensor_copy(h0m[:, :, 0:1], posb[:, m:m + 1, 0:1].broadcast_to([P, TI, 1]))
                last.then_inc(h0_done, 1)
                for k in range(TAPS - 1):
                    for c in range(KI):
                        if k == 0:
                            dve.wait_ge(xpad_done, KI * i + c + 1)
                            dve.wait_ge(tap_done, KI * i + c + 1)
                        else:
                            dve.wait_ge(conv_done, CONV_OPS * i + KI * (k - 1) + c + 1)
                        convc = conv[:, c, :].rearrange("p (a t) -> p a t", a=TI)
                        nc.vector.scalar_tensor_tensor(convc, xpad[:, c, :, k:k + TOKENS], convw[:, c, k:k + 1],
                                                       convc, ALU.mult, ALU.add).then_inc(conv_done, 1)
                for b in range(2):
                    dve.wait_ge(z_tanh, 2 * i + b + 1)
                    nc.vector.scalar_tensor_tensor(z2[:, 2 * b:2 * b + 2, :], half_tanh_z[:, 2 * b:2 * b + 2, :], 1.0,
                                                   two(BC[b]), ALU.add, ALU.mult).then_inc(z2_done, 1)
                dve.wait_ge(conv_tanh, i + 1)
                nc.vector.scalar_tensor_tensor(x2[:], half_tanh[:], 1.0, conv[:], ALU.add, ALU.mult).then_inc(x2_done, 1)
                dve.wait_ge(rows_done, i + 1)
                split(2 * i, W, bc_rows)
                dve.wait_ge(soft_step, 3 * i + 2)
                nc.vector.tensor_scalar(small[:], soft[:], SMALL, None, ALU.min).then_inc(small_done, 1)
                dve.wait_ge(series_done, i + 1)
                nc.vector.tensor_tensor(small[:], small[:], series[:], ALU.mult).then_inc(softplus_step, 1)
                dve.wait_ge(soft_step, 3 * i + 3)
                nc.vector.tensor_scalar(soft[:], soft[:], ln_small[:], ln_small[:], ALU.max,
                                        ALU.subtract).then_inc(softplus_step, 1)
                dve.wait_ge(softplus_step, 3 * i + 2)
                nc.vector.tensor_tensor(soft[:], soft[:], small[:], ALU.add).then_inc(softplus_step, 1)
                dve.wait_ge(softplus_step, 3 * i + 3)
                nc.vector.tensor_tensor(delta[:], delta[:], soft[:], ALU.add).then_inc(delta_done, 1)
                dve.wait_ge(delta_done, i + 1)
                nc.vector.scalar_tensor_tensor(du[:], x2[:], 0.5, delta[:], ALU.mult, ALU.mult).then_inc(du_done, 1)
                dve.wait_ge(du_done, i + 1)

            def shared_expert(i):
                dve.wait_ge(shared_tanh, i)
                nc.vector.scalar_tensor_tensor(act_s[:], tanh_s[:], 1.0, GU[1][:, 0:N], ALU.add,
                                               ALU.mult).then_inc(shared_step, 1)
                dve.wait_ge(shared_step, 2 * (i - 1) + 1)
                nc.vector.scalar_tensor_tensor(hid_s[:], act_s[:], 0.5, GU[1][:, N:2 * N], ALU.mult,
                                               ALU.mult).then_inc(shared_step, 1)

            def step(i, s, q, mamba, moe):
                g = STATES * i + s
                m = STATES * (i - 1) + s
                if mamba:
                    dve.wait_ge(bc_done, g + 1)
                    nc.vector.tensor_tensor(drive[q][:], du[:], BC[q][:, None, 0:N].broadcast_to([P, KI, N]),
                                            ALU.mult).then_inc(drive_done, 1)
                if moe:
                    dve.wait_ge(tanh_done, m + 1)
                    nc.vector.scalar_tensor_tensor(act_g[:], tanh_g[:], 1.0, two(GU[0]), ALU.add,
                                                   ALU.mult).then_inc(act_done, 1)
                if mamba:
                    dve.wait_ge(decay_done, g + 1)
                    dve.wait_ge(drive_done, g + 1)
                    nc.vector.tensor_tensor_scan(state[q][:].rearrange("p c n -> p (c n)"),
                                                 decay[q][:].rearrange("p a t -> p (a t)"),
                                                 drive[q][:].rearrange("p c n -> p (c n)"), 0.0,
                                                 ALU.mult, ALU.add).then_inc(decay_free, 1)
                if moe:
                    dve.wait_ge(act_done, m + 1)
                    nc.vector.tensor_tensor(hid[:], act_g[:], two(GU[1]), ALU.mult).then_inc(gu_free, 1)
                if mamba:
                    dve.wait_ge(decay_free, g + 3)
                    dve.wait_ge(read_free, g + 1)
                    nc.vector.tensor_tensor(read[q][:], state[q][:], BC[q][:, None, N:2 * N].broadcast_to([P, KI, N]),
                                            ALU.mult).then_inc(bc_free, 1)
                if moe:
                    dve.wait_ge(gu_free, m + 2)
                    dve.wait_ge(wb_done, m + 1)
                    dve.wait_ge(hidw_free, m + 1)
                    nc.vector.tensor_tensor(hidw[q][:], hid[:], two(W), ALU.mult).then_inc(wb_free, 1)

            def norm(no, source, to):
                dve.wait_ge(mean_done, no + 1)
                nc.vector.tensor_tensor(centred[:], source[:], GU[1][:, None, 0:N].broadcast_to([P, KM, N]),
                                        ALU.subtract).then_inc(centred_done, 1)
                dve.wait_ge(rough_step, 2 * no + 2)
                base = 4 * no
                nc.vector.scalar_tensor_tensor(newton[:, 0, :], W[:, 0:N], EPS, rough[:], ALU.add,
                                               ALU.mult).then_inc(newton_step, 1)
                dve.wait_ge(newton_step, base + 1)
                nc.vector.tensor_tensor(newton[:, 1, :], newton[:, 0, :], rough[:], ALU.mult).then_inc(newton_step, 1)
                dve.wait_ge(newton_step, base + 2)
                nc.vector.tensor_scalar(newton[:, 0, :], newton[:, 1, :], -0.5, 1.5, ALU.mult,
                                        ALU.add).then_inc(newton_step, 1)
                dve.wait_ge(newton_step, base + 3)
                nc.vector.tensor_tensor(rstd[:], newton[:, 0, :], rough[:], ALU.mult).then_inc(newton_step, 1)
                dve.wait_ge(newton_step, base + 4)
                nc.vector.tensor_tensor(to[:], centred[:], rstd[:, None, :].broadcast_to([P, KM, N]),
                                        ALU.mult).then_inc(norm_done, 1)

            def router(i):
                done = [0]

                def in_turn(ins):
                    done[0] += 1
                    ins.then_inc(route_step, 1)
                    dve.wait_ge(route_step, ROUTE * i + done[0])

                def gate():
                    dve.sem_inc(route_gate, 1)

                dve.wait_ge(ex_done, i + 1)
                in_turn(nc.vector.tensor_scalar(ex[:], ex[:], 1.0, None, ALU.add))
                in_turn(nc.vector.reciprocal(score[:], ex[:]))
                in_turn(nc.vector.tensor_reduce(gsum[:, :, 0:GROUPS],
                                                score[:].rearrange("p b (g e) -> p b g e", g=GROUPS), AX.X, ALU.add))
                for b in range(2):
                    gate()
                    in_turn(nc.vector.max(gtop[:, b, :], gsum[:, b, :]))
                in_turn(nc.vector.tensor_copy(glist[:, :, 0:TOPG], gtop[:, :, 0:TOPG]))
                for b in range(2):
                    gate()
                    in_turn(nc.vector.match_replace(gleft[:, b, :], glist[:, b, :], gsum[:, b, :], -1.0))
                in_turn(nc.vector.tensor_scalar(gmask[:], gleft[:, :, 0:GROUPS], -1.0, None, ALU.is_equal))
                in_turn(nc.vector.tensor_tensor(
                    masked[:].rearrange("p b (g e) -> p b g e", g=GROUPS), score[:].rearrange("p b (g e) -> p b g e", g=GROUPS),
                    gmask[:, :, :, None].broadcast_to([NB, 2, GROUPS, PER_GROUP]), ALU.mult))
                for b in range(2):
                    gate()
                    in_turn(nc.vector.max(etop[:, b, :], masked[:, b, :]))
                for b in range(2):
                    gate()
                    in_turn(nc.vector.match_replace(eleft[:, b, :], etop[:, b, :], masked[:, b, :], -1.0))
                in_turn(nc.vector.scalar_tensor_tensor(wsel[:], eleft[:], -1.0, masked[:], ALU.is_equal, ALU.mult))
                in_turn(nc.vector.tensor_reduce(wsum[:], wsel[:], AX.X, ALU.add))
                in_turn(nc.vector.tensor_scalar(wsum[:], wsum[:], 1e-12, None, ALU.max))
                in_turn(nc.vector.reciprocal(winv[:], wsum[:]))
                for b in range(2):
                    last = nc.vector.tensor_scalar(w3[:, b], wsel[:, b:b + 1, :].broadcast_to([NB, 3, EXPERTS]),
                                                   winv[:, b:b + 1], 0.5, ALU.mult, ALU.mult)
                last.then_inc(route_step, 1)
                assert done[0] + 1 == ROUTE, done

            def tile(i, mamba, moe):
                if mamba:
                    prologue(i)
                if moe:
                    shared_expert(i)
                with dve.Fori(0, PAIRS) as p:
                    for q in range(2):
                        step(i, 2 * p + q, q, mamba, moe)
                if moe:
                    dve.wait_ge(hidw_free, STATES * i + 2)
                    nc.vector.tensor_tensor(r2[:], two(O), h1[:], ALU.add).then_inc(r_done, 1)
                    dve.wait_ge(out_sent, 16 * i)
                    norm(norm_no(i, 1), r2, outb)
                if mamba:
                    dve.wait_ge(read_free, STATES * i + STATES + 2)
                    for b in range(2):
                        nc.vector.scalar_tensor_tensor(gated[:, 2 * b:2 * b + 2, :], two(Y[b]), 0.5,
                                                       z2[:, 2 * b:2 * b + 2, :], ALU.mult, ALU.mult).then_inc(gated_done, 1)
                    dve.wait_ge(outproj_done, i + 1)
                    nc.vector.tensor_tensor(r1[:], two(GU[0]), h0[:], ALU.add).then_inc(r_done, 1)
                    norm(norm_no(i, 0), r1, h1)
                    router(i)
                    dve.wait_ge(w3_turned, i + 1)
                    split(2 * i + 1, BC[0], w_rows)

            tiles(dve, tile)


def kernel(**inputs):
    import numpy as _np
    import concourse.bacc as _bacc
    from concourse import mybir as _mybir
    from concourse.bass_utils import run_bass_kernel_spmd as _run

    a = {k: _np.asarray(v) for k, v in inputs.items()}

    def rows(w):
        w = w.reshape(w.shape[0] // P, P, *w.shape[1:])
        return w.transpose(1, 0, *range(2, w.ndim))

    x = _np.zeros((TILES * TI, CHANNELS, GRID, PATCH, GRID, PATCH), a["x"].dtype)
    x[:IMAGES] = a["x"].reshape(IMAGES, CHANNELS, GRID, PATCH, GRID, PATCH)
    x = x.reshape(TILES, TI, CHANNELS, GRID, PATCH, GRID, PATCH).transpose(0, 2, 4, 6, 1, 3, 5)
    x = x.reshape(TILES, KF, P, NP).transpose(0, 2, 1, 3)

    def expert(gate, up, down):
        e = gate.shape[0]
        g, u = (w.transpose(0, 2, 1).reshape(e, KM, P, HID).transpose(0, 2, 1, 3).reshape(e, P, KM * HID)
                for w in (gate, up))
        return _np.concatenate([g, u, down.transpose(0, 2, 1)], axis=2)

    given = {
        "x": x,
        "w_tok": rows(a["L0_tok_W"].T),
        "b_tok": rows(a["L0_tok_b"]),
        "cls_tok": rows(a["L0_tok_cls_token"].reshape(DM)),
        "pos": rows(a["L0_tok_pos_enc"][0].T),
        "w_in": rows(a["L0_attn_W_in"].T),
        "conv_w": rows(a["L0_attn_conv_w"][:, 0, :]),
        "conv_b": rows(a["L0_attn_conv_b"]),
        "w_x": rows(a["L0_attn_W_x"].T),
        "w_dt": rows(a["L0_attn_W_dt"][:, 0]),
        "b_dt": rows(a["L0_attn_b_dt"]),
        "a_log": rows(a["L0_attn_A_log"]).reshape(P, KI * STATES),
        "d_par": rows(a["L0_attn_D_param"]),
        "w_out": rows(a["L0_attn_W_out"].T),
        "gate_w": rows(a["L0_ffn_gate_w"].T),
        "experts": expert(a["L0_ffn_expert_gate"], a["L0_ffn_expert_up"], a["L0_ffn_expert_down"]),
        "shared": expert(*(a[f"L0_ffn_shared_{n}_w"][None] for n in ("gate", "up", "down")))[0],
    }
    nc = _bacc.Bacc("TRN2", target_bir_lowering=False, num_devices=1)
    arrays, args = {}, []
    for name, v in given.items():
        v = _np.ascontiguousarray(v)
        arrays[f"in_{name}_dram"] = v
        args.append(nc.dram_tensor(f"in_{name}_dram", v.shape, _mybir.dt.from_np(v.dtype), kind="ExternalInput").ap())
    args.append(nc.dram_tensor("out_dram", (TILES, P, KM, N), _mybir.dt.float32, kind="ExternalOutput").ap())
    build(nc, *args)
    r = _run(nc, [arrays], core_ids=[0])
    got = r.results[0]["out_dram"].reshape(TILES, P, KM, TI, TOKENS).transpose(0, 3, 4, 2, 1)
    return _np.ascontiguousarray(got.reshape(TILES * TI, TOKENS, DM)[:IMAGES])
```

```python
from contextlib import ExitStack

import concourse.bass as bass
from concourse import mybir

F32 = mybir.dt.float32
F32R = mybir.dt.float32r
BF16 = mybir.dt.bfloat16
ALU = mybir.AluOpType
ACT = mybir.ActivationFunctionType
AX = mybir.AxisListType

P = 128
IMAGES, CHANNELS, SIDE, PATCH = 64, 3, 96, 16
GRID = SIDE // PATCH
PATCHES = GRID * GRID
TOKENS = PATCHES + 1
FEATS = CHANNELS * PATCH * PATCH
DM, DI, STATES, TAPS = 256, 512, 16, 4
EXPERTS, TOPK, GROUPS, TOPG, HID = 32, 8, 8, 4, 128
PER_GROUP = EXPERTS // GROUPS
TI = 6
TILES = -(-IMAGES // TI)
N = TI * TOKENS
NB = N // 2
NP = TI * PATCHES
KF, KM, KI = FEATS // P, DM // P, DI // P
PADT = TOKENS + TAPS - 1
ROWS = 2 * STATES
SPLIT = 3 * ROWS
GCOLS = 4 * P
WCOLS = GCOLS + DM
PAIRS = EXPERTS // 2
EARLY = 2
ROUNDS = 4
SETS = 3
SCANS = STATES // ROUNDS
IN_SET = [5, 6, 5]
FIRST, SECOND, LAST_BUT_ONE, LAST = (-1, 1), (-1, 2), (ROUNDS, 0), (ROUNDS, 1)


def pair_no(p, k):
    return EARLY + SETS * p + k


def uses(t, p, k):
    return IN_SET[k] * t + p + (1 if k else 0)


def split_no(p, k):
    return 1 - pair_no(p, k) if isinstance(p, int) and p < 0 else pair_no(p, k)


def ready_no(p, k):
    return 1 if isinstance(p, int) and p < 0 else pair_no(p, k)


def two_on(p, k):
    return (p, k + 2) if k == 0 else (p + 1, k - 1)


EPS = 1e-5
SMALL = 2.0 ** -11


def build(nc, x, w_tok, b_tok, cls_tok, pos, w_in, conv_w, conv_b, w_x, w_dt, b_dt, a_log, d_par, w_out,
          gate_w, experts_gu, experts_down, shared, out):
    with ExitStack() as ctx:
        def sb(name, shape, dt=F32):
            return ctx.enter_context(nc.sbuf_tensor(name, shape, dt))

        def ps(name):
            return ctx.enter_context(nc.psum_tensor(name, [P, 512], F32))

        def sem(name):
            return ctx.enter_context(nc.semaphore(name))

        tokw = sb("tokw", [P, KF, DM])
        inw = sb("inw", [P, KM, 2 * DI])
        outw = sb("outw", [P, KI, DM])
        gatew = sb("gatew", [P, KM, EXPERTS])
        sharedw = sb("sharedw", [P, WCOLS])
        xw_raw = sb("xw_raw", [P, KI, 1 + ROWS])
        xw = sb("xw", [P, KI, 3, ROWS])
        dtw = sb("dtw", [P, KI, P])
        posb = sb("posb", [P, KM, TOKENS])
        tokb = sb("tokb", [P, KM])
        clsb = sb("clsb", [P, KM])
        convw = sb("convw", [P, KI, TAPS])
        convb = sb("convb", [P, KI])
        dt_scale = sb("dt_scale", [P, KI])
        dt_bias = sb("dt_bias", [P, KI])
        alog = sb("alog", [P, KI * STATES])
        aexp = sb("aexp", [P, KI * STATES])
        aneg = sb("aneg", [P, STATES, KI])
        dpar = sb("dpar", [P, KI])
        ident = sb("ident", [P, P])
        diag_d = sb("diag_d", [P, KI, P])
        averager = sb("averager", [P, P])
        sel = sb("sel", [SPLIT, ROWS, P], BF16)
        one_col = sb("one_col", [P, 1])
        eps_col = sb("eps_col", [P, 1])
        small_col = sb("small_col", [P, 1])
        ln_small = sb("ln_small", [P, 1])

        patches = sb("patches", [P, KF, NP])
        h0 = sb("h0", [P, KM, N])
        xpad = sb("xpad", [P, KI, TI, PADT])
        conv = sb("conv", [P, KI, N])
        half_tanh = sb("half_tanh", [P, KI, N])
        half_tanh_z = sb("half_tanh_z", [P, KI, N])
        x2 = sb("x2", [P, KI, N])
        z2 = sb("z2", [P, KI, N])
        delta = sb("delta", [P, KI, N])
        soft = sb("soft", [P, KI, N])
        du = sb("du", [P, KI, N])
        bc_rows = sb("bc_rows", [SPLIT, N], BF16)
        w_rows = sb("w_rows", [SPLIT, N], BF16)
        rest = sb("rest", [SPLIT, N])
        mid = sb("mid", [SPLIT, N], BF16)
        decay = [sb(f"decay{q}", [P, KI * TI, TOKENS]) for q in range(2)]
        drive = [sb(f"drive{q}", [P, KI, N]) for q in range(2)]
        state = [sb(f"state{q}", [P, KI, N]) for q in range(2)]
        read = [sb(f"read{q}", [P, KI, N]) for q in range(SCANS)]
        gated = sb("gated", [P, KI, N])
        small, series = drive[1], read[1]
        r1 = sb("r1", [P, KM, N])
        r2 = sb("r2", [P, KM, N])
        centred = sb("centred", [P, KM, N])
        squared = sb("squared", [P, KM, N])
        var_eps = sb("var_eps", [P, N])
        rough = sb("rough", [P, N])
        newton = sb("newton", [P, 2, N])
        rstd = sb("rstd", [P, N])
        h1 = sb("h1", [P, KM, N])
        h1_kept = sb("h1_kept", [P, KM, N])
        h1_hi = sb("h1_hi", [P, KM, N], F32R)
        h1_lo = sb("h1_lo", [P, KM, N], F32R)
        outb = sb("outb", [P, KM, N])

        ex = sb("ex", [NB, 2, EXPERTS])
        score = sb("score", [NB, 2, EXPERTS])
        gsum = sb("gsum", [NB, 2, GROUPS + 8 - TOPG])
        gtop = sb("gtop", [NB, 2, 8])
        glist = sb("glist", [NB, 2, 8])
        gleft = sb("gleft", [NB, 2, GROUPS + 8 - TOPG])
        gmask = sb("gmask", [NB, 2, GROUPS])
        masked = sb("masked", [NB, 2, EXPERTS])
        etop = sb("etop", [NB, 2, 8])
        eleft = sb("eleft", [NB, 2, EXPERTS])
        wsel = sb("wsel", [NB, 2, EXPERTS])
        wsum = sb("wsum", [NB, 2])
        winv = sb("winv", [NB, 2])
        w3 = sb("w3", [NB, 2, 3, EXPERTS])

        raw = [sb(f"raw{k}", [P, 2, GCOLS]) for k in range(SETS)]
        guw_hi = [sb(f"guw_hi{k}", [P, 2, GCOLS], F32R) for k in range(SETS)]
        guw_lo = [sb(f"guw_lo{k}", [P, 2, GCOLS], F32R) for k in range(SETS)]
        downw = [sb(f"downw{k}", [P, 2, DM]) for k in range(SETS)]
        sharedw_hi = sb("sharedw_hi", [P, GCOLS], F32R)
        sharedw_lo = sb("sharedw_lo", [P, GCOLS], F32R)
        tanh_g = sb("tanh_g", [P, 2, N])
        act_g = sb("act_g", [P, 2, N])
        hid = [sb(f"hid{k}", [P, 2, N]) for k in range(SETS)]
        spread_w = [sb(f"spread_w{k}", [P, 2, N]) for k in range(SETS)]
        hidw = [sb(f"hidw{k}", [P, 2, N]) for k in range(SETS)]
        tanh_s = sb("tanh_s", [P, N])
        act_s = sb("act_s", [P, N])
        hid_s = sb("hid_s", [P, N])

        Y = [ps("Y0"), ps("Y1")]
        GU = [ps("GU0"), ps("GU1")]
        BC = [ps("BC0"), ps("BC1")]
        O = ps("O")
        W = ps("W")

        def two(bank):
            return bank[:, 0:2 * N].rearrange("p (c n) -> p c n", c=2)

        weights_in = sem("weights_in")
        consts_pool = sem("consts_pool")
        aexp_done = sem("aexp_done")
        consts_dve = sem("consts_dve")
        setup_done = sem("setup_done")
        patches_in = sem("patches_in")
        tok_done = sem("tok_done")
        h0_done = sem("h0_done")
        xz_done = sem("xz_done")
        xpad_done = sem("xpad_done")
        tap_done = sem("tap_done")
        conv_done = sem("conv_done")
        conv_tanh = sem("conv_tanh")
        z_tanh = sem("z_tanh")
        x2_done = sem("x2_done")
        z2_done = sem("z2_done")
        dt_done = sem("dt_done")
        rows_done = sem("rows_done")
        bc_split = sem("bc_split")
        w_split = sem("w_split")
        soft_step = sem("soft_step")
        small_done = sem("small_done")
        series_done = sem("series_done")
        product_done = sem("product_done")
        softplus_step = sem("softplus_step")
        delta_done = sem("delta_done")
        du_done = sem("du_done")
        y_init = sem("y_init")
        bc_done = sem("bc_done")
        decay_done = sem("decay_done")
        drive_done = sem("drive_done")
        decay_free = sem("decay_free")
        bc_free = sem("bc_free")
        sum_ready = sem("sum_ready")
        sum_free = sem("sum_free")
        gated_done = sem("gated_done")
        outproj_done = sem("outproj_done")
        def norm_sems(of):
            return {n: sem(f"{of}_{n}") for n in ("sum", "mean", "centred", "squared", "var", "eps", "rough", "newton", "gate", "done")}

        mix_norm = norm_sems("mix_norm")
        out_norm = norm_sems("out_norm")
        logits_done = sem("logits_done")
        ex_done = sem("ex_done")
        route_step = sem("route_step")
        route_gate = sem("route_gate")
        w3_turned = sem("w3_turned")
        shared_gu = sem("shared_gu")
        shared_tanh = sem("shared_tanh")
        shared_step = sem("shared_step")
        shared_down = sem("shared_down")
        h1_hi_done = sem("h1_hi_done")
        h1_kept_done = sem("h1_kept_done")
        h1_lo_done = sem("h1_lo_done")
        raw_in = [sem(f"raw_in{k}") for k in range(SETS)]
        downw_in = [sem(f"downw_in{k}") for k in range(SETS)]
        hi_done = sem("hi_done")
        lo_done = sem("lo_done")
        gu_done = sem("gu_done")
        tanh_done = sem("tanh_done")
        act_done = sem("act_done")
        gu_free = sem("gu_free")
        wb_done = sem("wb_done")
        wb_free = sem("wb_free")
        weighted = sem("weighted")
        hidw_free = sem("hidw_free")
        out_sent = sem("out_sent")

        LOADS = [(tokw, w_tok), (inw, w_in), (outw, w_out), (gatew, gate_w), (sharedw, shared), (xw_raw, w_x),
                 (posb, pos), (tokb, b_tok), (clsb, cls_tok), (convw, conv_w), (convb, conv_b),
                 (dt_scale, w_dt), (dt_bias, b_dt), (alog, a_log), (dpar, d_par)]
        CONSTS_POOL = 11
        CONV_OPS = KI * (TAPS - 1)
        SPLITS = 4
        ROUTE = 19
        LNS = 2

        def periods(eng, scans, turn):
            turn(-1, False, False, True)
            scans(0, True, False)
            turn(0, True, False, True)
            with eng.Fori(1, TILES - 1) as i:
                scans(i, True, True)
                turn(i, True, True, True)
            scans(TILES - 1, True, True)
            turn(TILES - 1, True, True, False)
            scans(TILES, False, True)
            turn(TILES, False, True, False)

        def pair_index(t, p, k):
            return PAIRS * t + pair_no(p, k)

        def set_credit(t, p, k):
            return pair_index(t, p, k) + (SETS if isinstance(p, int) and (p, k) == FIRST else 1)

        def normalise(eng, ops, no, sems, to):
            eng.wait_ge(sems["rough"], 2 * no + 2)
            ops.tensor_tensor(newton[:, 0, :], var_eps[:], rough[:], ALU.mult).then_inc(sems["newton"], 1)
            eng.wait_ge(sems["newton"], 4 * no + 1)
            ops.tensor_tensor(newton[:, 1, :], newton[:, 0, :], rough[:], ALU.mult).then_inc(sems["newton"], 1)
            eng.wait_ge(sems["newton"], 4 * no + 2)
            eng.sem_inc(sems["gate"], 1)
            ops.tensor_scalar(newton[:, 0, :], newton[:, 1, :], -0.5, 1.5, ALU.mult, ALU.add).then_inc(sems["newton"], 1)
            eng.wait_ge(sems["newton"], 4 * no + 3)
            ops.tensor_tensor(rstd[:], newton[:, 0, :], rough[:], ALU.mult).then_inc(sems["newton"], 1)
            eng.wait_ge(sems["newton"], 4 * no + 4)
            ops.tensor_tensor(to[:], centred[:], rstd[:, None, :].broadcast_to([P, KM, N]),
                              ALU.mult).then_inc(sems["done"], 1)

        block = ctx.enter_context(nc.Block())

        @block.sync
        def _(sp):
            sp.sem_inc(out_sent, 16)
            for to, of in LOADS:
                sp.dma_start(to[:], of).then_inc(weights_in, 16)
            sp.dma_start(patches[:], x[0]).then_inc(patches_in, 16)

            def load_raw(t, p, k):
                sp.wait_ge(lo_done, PAIRS * t + split_no(p, k) + 1)
                sp.dma_start(raw[k][:], experts_gu[pair_no(p, k)]).then_inc(raw_in[k], 16)

            def load_down(t, p, k):
                sp.wait_ge(hidw_free, set_credit(t, p, k))
                sp.dma_start(downw[k][:], experts_down[pair_no(p, k)]).then_inc(downw_in[k], 16)

            def load_patches(t):
                sp.wait_ge(tok_done, t)
                sp.dma_start(patches[:], x[t]).then_inc(patches_in, 16)

            def send(t):
                sp.wait_ge(out_norm["done"], t + 1)
                sp.dma_start(out[t], outb[:]).then_inc(out_sent, 16)

            def tile(t, first, more):
                load_raw(t, *SECOND)
                if not first:
                    load_down(t - 1, *LAST_BUT_ONE)
                load_raw(t, *FIRST)
                if not first:
                    load_down(t - 1, *LAST)
                load_raw(t, 0, 0)
                load_down(t, *FIRST)
                load_raw(t, 0, 1)
                load_down(t, *SECOND)
                if more:
                    load_patches(t + 2)
                with sp.Fori(0, ROUNDS - 1) as p:
                    load_raw(t, p, 2)
                    load_down(t, p, 0)
                    load_raw(t, p + 1, 0)
                    load_down(t, p, 1)
                    load_raw(t, p + 1, 1)
                    load_down(t, p, 2)
                load_raw(t, ROUNDS - 1, 2)
                load_down(t, ROUNDS - 1, 0)
                load_raw(t, ROUNDS, 0)
                load_down(t, ROUNDS - 1, 1)
                load_raw(t, ROUNDS, 1)
                load_down(t, ROUNDS - 1, 2)
                if not first:
                    send(t - 1)

            load_patches(1)
            tile(0, True, True)
            with sp.Fori(1, TILES - 2) as t:
                tile(t, False, True)
            tile(TILES - 2, False, False)
            tile(TILES - 1, False, False)
            load_down(TILES - 1, *LAST_BUT_ONE)
            load_down(TILES - 1, *LAST)
            send(TILES - 1)
            sp.wait_ge(out_sent, 16 * (TILES + 1))

        @block.gpsimd
        def _(pool):
            nc.gpsimd.memset(ident[:], 0.0).then_inc(consts_pool, 1)
            nc.gpsimd.memset(sel[:], 0.0).then_inc(consts_pool, 1)
            pool.wait_ge(consts_pool, 2)
            nc.gpsimd.affine_select(out=ident[:], in_=ident[:], compare_op=ALU.not_equal, fill=1.0, base=0,
                                    pattern=[[-1, P]], channel_multiplier=1).then_inc(consts_pool, 1)
            for part in range(3):
                nc.gpsimd.affine_select(out=sel[:], in_=sel[:], compare_op=ALU.not_equal, fill=1.0,
                                        base=-ROWS * part, pattern=[[-1, ROWS], [0, P]],
                                        channel_multiplier=1).then_inc(consts_pool, 1)
                pool.wait_ge(consts_pool, 4 + part)
            nc.gpsimd.memset(xpad[:], 0.0).then_inc(consts_pool, 1)
            for q in range(2):
                nc.gpsimd.memset(decay[q][:], 0.0).then_inc(consts_pool, 1)
            nc.gpsimd.memset(glist[:], -2.0).then_inc(consts_pool, 1)
            nc.gpsimd.memset(gsum[:], -2.0).then_inc(consts_pool, 1)
            pool.sem_inc(lo_done, 2)

            def low_part(t, p, k):
                pool.wait_ge(hi_done, PAIRS * t + split_no(p, k) + 1)
                nc.gpsimd.tensor_tensor(guw_lo[k][:], raw[k][:], guw_hi[k][:].bitcast(F32), ALU.subtract).then_inc(lo_done, 1)

            def weight(t, p, k):
                g = pair_index(t, p, k)
                pool.wait_ge(gu_free, 2 * g + 4)
                pool.wait_ge(wb_free, g + 2)
                pool.wait_ge(hidw_free, set_credit(t, p, k))
                nc.gpsimd.tensor_tensor(hidw[k][:], hid[k][:], spread_w[k][:], ALU.mult).then_inc(weighted, 1)

            def sum_pair(i, p, r):
                pool.wait_ge(bc_free, STATES * i + SCANS * p + 2 * r + 4)
                nc.gpsimd.tensor_tensor(read[2 * r][:], read[2 * r][:], read[2 * r + 1][:], ALU.add).then_inc(sum_ready, 1)

            def scans(i, mixer, experts):
                with pool.Fori(0, ROUNDS) as p:
                    for k in range(SCANS):
                        if mixer and k % 2:
                            sum_pair(i, p, k // 2)
                        if experts and k < SETS:
                            weight(i - 1, p, k)
                            low_part(i - 1, *two_on(p, k))

            def token_low_part(i):
                pool.wait_ge(h1_hi_done, i + 1)
                nc.gpsimd.tensor_tensor(h1_lo[:], h1[:], h1_hi[:].bitcast(F32), ALU.subtract).then_inc(h1_lo_done, 1)

            def turn(i, end, old, nxt):
                t, n = i - 1, i + 1
                if old:
                    weight(t, *LAST_BUT_ONE)
                if end:
                    low_part(i, *SECOND)
                if old:
                    weight(t, *LAST)
                if end:
                    low_part(i, *FIRST)
                    token_low_part(i)
                if nxt:
                    pool.wait_ge(series_done, n + 1)
                    nc.gpsimd.tensor_tensor(small[:], small[:], series[:], ALU.mult).then_inc(product_done, 1)
                if end:
                    low_part(i, 0, 0)
                    weight(i, *FIRST)
                    weight(i, *SECOND)
                    low_part(i, 0, 1)
                if old:
                    pool.wait_ge(out_sent, 16 * (t + 1))
                    normalise(pool, nc.gpsimd, t, out_norm, outb)

            periods(pool, scans, turn)

        @block.tensor
        def _(pe):
            pe.sem_inc(hidw_free, SETS)
            pe.sem_inc(sum_free, 2)
            pe.wait_ge(weights_in, 16 * len(LOADS))
            pe.wait_ge(consts_pool, CONSTS_POOL)
            pe.wait_ge(setup_done, 1)

            def project_patches(i, m):
                pe.wait_ge(patches_in, 16 * (i + 1))
                for k in range(KF):
                    mm = nc.tensor.matmul(BC[0][:, m * NP:(m + 1) * NP], tokw[:, k, m * P:(m + 1) * P],
                                          patches[:, k, :], start=(k == 0), stop=(k == KF - 1))
                if m == KM - 1:
                    mm.then_inc(tok_done, 1)

            X_BANKS, Z_BANKS = (Y[1], BC[1]), (BC[0], Y[0])

            def project_in(i, first_chunk, banks):
                for c in range(KI):
                    for k in range(KM):
                        at = first_chunk + c
                        mm = nc.tensor.matmul(banks[c // 2][:, (c % 2) * N:(c % 2 + 1) * N], inw[:, k, at * P:(at + 1) * P],
                                              h0[:, k, :], start=(k == 0), stop=(k == KM - 1))
                    if c % 2:
                        mm.then_inc(xz_done, 1)

            def project_x(i):
                pe.wait_ge(x2_done, 2 * i + 2)
                pe.wait_ge(z2_done, 2 * i + 2)
                for c in range(KI):
                    mm = nc.tensor.matmul(BC[0][:, 0:N], dtw[:, c, :], x2[:, c, :], start=(c == 0), stop=(c == KI - 1))
                mm.then_inc(dt_done, 1)
                for c in range(KI):
                    mm = nc.tensor.matmul(BC[1][0:SPLIT, 0:N], xw[:, c].rearrange("p a b -> p (a b)"), x2[:, c, :],
                                          start=(c == 0), stop=(c == KI - 1))
                mm.then_inc(rows_done, 1)
                for c in range(KI):
                    mm = nc.tensor.matmul(Y[c // 2][:, (c % 2) * N:(c % 2 + 1) * N], diag_d[:, c, :], x2[:, c, :],
                                          start=(c % 2 == 0), stop=False, skip_group_check=True)

            def products(bank, at, high, low, column, hi_in, lo_in):
                passes = [(w, v) for w, v in ((high, hi_in), (high, lo_in), (low, hi_in))]
                for n, (w, v) in enumerate(passes):
                    for k in range(KM):
                        mm = nc.tensor.matmul(bank[:, at:at + N], w[:, (column + k) * P:(column + k + 1) * P], v[:, k, :],
                                              start=(n == 0 and k == 0), stop=(n == 2 and k == KM - 1))
                return mm

            def shared_gate_up(t):
                pe.wait_ge(h1_hi_done, t + 1)
                pe.wait_ge(h1_lo_done, t + 1)
                for g in range(2):
                    mm = products(GU[g], 0, sharedw_hi, sharedw_lo, 2 * g, h1_hi, h1_lo)
                mm.then_inc(shared_gu, 1)

            def shared_out(t):
                pe.wait_ge(shared_step, 2 * t + 2)
                for m in range(KM):
                    mm = nc.tensor.matmul(O[:, m * N:(m + 1) * N], sharedw[:, (4 + m) * P:(5 + m) * P], hid_s[:],
                                          start=(m == 0), stop=False, skip_group_check=True)

            def spread_bc(i, s, q):
                pe.wait_ge(bc_free, STATES * i + s + 1)
                for j in range(2):
                    mm = nc.tensor.matmul(BC[q][:, j * N:(j + 1) * N], sel[:, STATES * j + s, :], bc_rows[:],
                                          start=True, stop=True)
                mm.then_inc(bc_done, 1)

            def gate_up(t, p, k):
                pe.wait_ge(lo_done, PAIRS * t + ready_no(p, k) + 3)
                for j in range(2):
                    pe.wait_ge(gu_free, 2 * pair_index(t, p, k) + j + 1)
                    for g in range(2):
                        mm = products(GU[j], g * N, guw_hi[k][:, j], guw_lo[k][:, j], 2 * g, h1_hi, h1_lo)
                    mm.then_inc(gu_done, 1)

            def spread_weights(t, p, k):
                pe.wait_ge(wb_free, pair_index(t, p, k) + 1)
                for j in range(2):
                    mm = nc.tensor.matmul(W[:, j * N:(j + 1) * N], sel[:, 2 * pair_no(p, k) + j, :], w_rows[:],
                                          start=True, stop=True)
                mm.then_inc(wb_done, 1)

            def down(t, p, k):
                pe.wait_ge(weighted, pair_index(t, p, k) + SETS + 1)
                pe.wait_ge(downw_in[k], 16 * (uses(t, p, k) + 1))
                for j in range(2):
                    for c in range(KM):
                        mm = nc.tensor.matmul(O[:, c * N:(c + 1) * N], downw[k][:, j, c * P:(c + 1) * P],
                                              hidw[k][:, j, :], start=False, stop=False, skip_group_check=True)
                mm.then_inc(hidw_free, 1)

            def sum_y(i, p, r):
                pe.wait_ge(sum_ready, STATES // 2 * i + SCANS // 2 * p + r + 1)
                for b in range(2):
                    mm = nc.tensor.matmul(Y[b][:, 0:2 * N], ident[:], read[2 * r][:, 2 * b:2 * b + 2, :].rearrange("p c n -> p (c n)"),
                                          start=False, stop=False, skip_group_check=True)
                mm.then_inc(sum_free, 1)

            def mean(no, sems, source, bank):
                pe.wait_ge(sems["sum"], no + 1)
                for k in range(KM):
                    mm = nc.tensor.matmul(bank[:, 0:N], averager[:], source[:, k, :], start=(k == 0), stop=(k == KM - 1))
                mm.then_inc(sems["mean"], 1)

            def variance(no, sems, bank):
                pe.wait_ge(sems["squared"], no + 1)
                for k in range(KM):
                    mm = nc.tensor.matmul(bank[:, 0:N], averager[:], squared[:, k, :], start=(k == 0), stop=(k == KM - 1))
                mm.then_inc(sems["var"], 1)

            def project_out(i):
                pe.wait_ge(gated_done, 2 * i + 2)
                for m in range(KM):
                    for c in range(KI):
                        mm = nc.tensor.matmul(Y[0][:, m * N:(m + 1) * N], outw[:, c, m * P:(m + 1) * P],
                                              gated[:, c, :], start=(c == 0), stop=(c == KI - 1))
                mm.then_inc(outproj_done, 1)

            def logits(i):
                pe.wait_ge(mix_norm["done"], i + 1)
                for b in range(2):
                    for k in range(KM):
                        mm = nc.tensor.matmul(W[0:NB, b * EXPERTS:(b + 1) * EXPERTS], h1[:, k, b * NB:(b + 1) * NB],
                                              gatew[:, k, :], start=(k == 0), stop=(k == KM - 1))
                mm.then_inc(logits_done, 1)

            def turn_weights(i):
                pe.wait_ge(route_step, ROUTE * (i + 1))
                for b in range(2):
                    mm = nc.tensor.transpose(W[0:SPLIT, b * NB:(b + 1) * NB],
                                             w3[:, b].rearrange("p a e -> p (a e)"), ident[0:NB, 0:NB])
                mm.then_inc(w3_turned, 1)

            def scans(i, mixer, experts):
                t = i - 1

                def one_round(p, first, final):
                    for k in range(SCANS):
                        if experts and k < SETS:
                            gate_up(t, p, k)
                            spread_weights(t, p, k)
                        if mixer and not (final and k == SCANS - 1):
                            spread_bc(i, SCANS * p + k + 1, 1 - k % 2)
                        if experts and k < SETS:
                            down(t, *((p, k - 1) if k else SECOND if first else (p - 1, 2)))
                        if mixer and k == 0 and not first:
                            sum_y(i, p - 1, 1)
                        if mixer and k == 2:
                            sum_y(i, p, 0)

                one_round(0, True, False)
                with pe.Fori(1, ROUNDS - 1) as p:
                    one_round(p, False, False)
                one_round(ROUNDS - 1, False, True)

            def turn(i, end, old, nxt):
                t, n = i - 1, i + 1
                if old:
                    gate_up(t, *LAST_BUT_ONE)
                    spread_weights(t, *LAST_BUT_ONE)
                    down(t, ROUNDS - 1, 2)
                if end:
                    sum_y(i, ROUNDS - 1, 1)
                if old:
                    down(t, *LAST_BUT_ONE)
                if end:
                    project_out(i)
                if nxt:
                    project_patches(n, 0)
                if end:
                    if old:
                        pe.wait_ge(wb_free, pair_index(t, *LAST_BUT_ONE) + 2)
                    mean(i, mix_norm, r1, W)
                if nxt:
                    project_patches(n, 1)
                if end:
                    variance(i, mix_norm, W)
                if old:
                    gate_up(t, *LAST)
                    if end:
                        pe.wait_ge(mix_norm["eps"], i + 1)
                    spread_weights(t, *LAST)
                if nxt:
                    pe.wait_ge(h0_done, n + 1)
                    project_in(n, 0, X_BANKS)
                if end:
                    if old:
                        pe.wait_ge(wb_free, pair_index(t, *LAST) + 2)
                    logits(i)
                if old:
                    down(t, *LAST)
                if nxt:
                    project_in(n, KI, Z_BANKS)
                if old:
                    mean(t, out_norm, r2, O)
                if end:
                    shared_gate_up(i)
                if old:
                    variance(t, out_norm, O)
                if nxt:
                    project_x(n)
                if end:
                    if old:
                        pe.wait_ge(out_norm["eps"], t + 1)
                    shared_out(i)
                    gate_up(i, *FIRST)
                    turn_weights(i)
                    gate_up(i, *SECOND)
                    pe.wait_ge(w_split, SPLITS * (i + 1))
                    spread_weights(i, *FIRST)
                if nxt:
                    pe.wait_ge(bc_split, SPLITS * (n + 1))
                    pe.wait_ge(soft_step, 3 * n + 1)
                    spread_bc(n, 0, 0)
                if end:
                    spread_weights(i, *SECOND)
                    down(i, *FIRST)

            periods(pe, scans, turn)

        @block.scalar
        def _(act):
            act.wait_ge(weights_in, 16 * len(LOADS))
            nc.scalar.activation(aexp[:], alog[:], ACT.Exp).then_inc(aexp_done, 1)
            act.wait_ge(consts_dve, 1)
            nc.scalar.activation(ln_small[:], small_col[:], ACT.Ln, bias=one_col[:]).then_inc(aexp_done, 1)
            nc.scalar.activation(sharedw_hi[:], sharedw[:, 0:GCOLS], ACT.Copy).then_inc(aexp_done, 1)
            act.wait_ge(consts_pool, CONSTS_POOL)
            act.wait_ge(setup_done, 1)

            X_BANKS, Z_BANKS = (Y[1], BC[1]), (BC[0], Y[0])

            def read_x(i):
                for b in range(2):
                    act.wait_ge(xz_done, 4 * i + b + 1)
                    for c in range(2 * b, 2 * b + 2):
                        src = X_BANKS[b][:, (c % 2) * N:(c % 2 + 1) * N]
                        nc.scalar.activation(xpad[:, c, :, TAPS - 1:PADT], src.rearrange("p (a t) -> p a t", a=TI),
                                             ACT.Copy).then_inc(xpad_done, 1)
                        nc.scalar.activation(conv[:, c, :], src, ACT.Identity, scale=convw[:, c, TAPS - 1:TAPS],
                                             bias=convb[:, c:c + 1]).then_inc(tap_done, 1)

            def tanh_z(i):
                for b in range(2):
                    act.wait_ge(xz_done, 4 * i + 3 + b)
                    nc.scalar.activation(half_tanh_z[:, 2 * b:2 * b + 2, :], two(Z_BANKS[b]), ACT.Tanh,
                                         scale=0.5).then_inc(z_tanh, 1)

            def tanh_conv(i):
                for b in range(2):
                    act.wait_ge(conv_done, CONV_OPS * i + CONV_OPS // 2 * (b + 1))
                    nc.scalar.activation(half_tanh[:, 2 * b:2 * b + 2, :], conv[:, 2 * b:2 * b + 2, :], ACT.Tanh,
                                         scale=0.5).then_inc(conv_tanh, 1)

            def softplus_exp(i):
                act.wait_ge(dt_done, i + 1)
                for c in range(KI):
                    nc.scalar.activation(soft[:, c, :], BC[0][:, 0:N], ACT.Abs, scale=dt_scale[:, c:c + 1],
                                         bias=dt_bias[:, c:c + 1])
                    last = nc.scalar.activation(delta[:, c, :], BC[0][:, 0:N], ACT.Relu, scale=dt_scale[:, c:c + 1],
                                                bias=dt_bias[:, c:c + 1])
                last.then_inc(soft_step, 1)
                act.wait_ge(soft_step, 3 * i + 1)
                nc.scalar.activation(soft[:], soft[:], ACT.Exp, scale=-1.0).then_inc(soft_step, 1)

            def softplus_ln(i):
                act.wait_ge(small_done, i + 1)
                nc.scalar.activation(series[:], small[:], ACT.Identity, scale=-0.5, bias=one_col[:]).then_inc(series_done, 1)
                nc.scalar.activation(soft[:], soft[:], ACT.Ln, bias=one_col[:]).then_inc(soft_step, 1)

            def decays(i, s, q):
                act.wait_ge(decay_free, STATES * i + s + 1)
                for c in range(KI):
                    last = nc.scalar.activation(
                        decay[q][:, c * TI:(c + 1) * TI, 1:TOKENS],
                        delta[:, c, :].rearrange("p (a t) -> p a t", a=TI)[:, :, 1:TOKENS],
                        ACT.Exp, scale=aneg[:, s, c:c + 1])
                last.then_inc(decay_done, 1)

            def high_part(t, p, k):
                act.wait_ge(raw_in[k], 16 * (uses(t, p, k) + 1))
                nc.scalar.activation(guw_hi[k][:], raw[k][:], ACT.Copy).then_inc(hi_done, 1)

            def gate_tanh(t, p, k):
                for j in range(2):
                    act.wait_ge(gu_done, 2 * pair_index(t, p, k) + j + 1)
                    nc.scalar.activation(tanh_g[:, j, :], GU[j][:, 0:N], ACT.Tanh, scale=0.5).then_inc(tanh_done, 1)

            def copy_weights(t, p, k):
                act.wait_ge(wb_done, pair_index(t, p, k) + 1)
                act.wait_ge(weighted, set_credit(t, p, k))
                nc.scalar.activation(spread_w[k][:], two(W), ACT.Copy).then_inc(wb_free, 1)

            def pair(t, p, k):
                gate_tanh(t, p, k)
                copy_weights(t, p, k)

            def square(no, sems):
                act.wait_ge(sems["centred"], no + 1)
                nc.scalar.activation(squared[:], centred[:], ACT.Square).then_inc(sems["squared"], 1)

            def read_variance(no, sems, bank):
                act.wait_ge(sems["var"], no + 1)
                nc.scalar.activation(var_eps[:], bank[:, 0:N], ACT.Identity, bias=eps_col[:]).then_inc(sems["eps"], 1)

            def rough_rstd(no, sems):
                act.wait_ge(sems["eps"], no + 1)
                nc.scalar.activation(rough[:], var_eps[:], ACT.Ln).then_inc(sems["rough"], 1)
                act.wait_ge(sems["rough"], 2 * no + 1)
                nc.scalar.activation(rough[:], rough[:], ACT.Exp, scale=-0.5).then_inc(sems["rough"], 1)

            def scans(i, mixer, experts):
                def one_round(p, final):
                    for k in range(SCANS):
                        if experts and k < SETS:
                            pair(i - 1, p, k)
                        if mixer and not (final and k == SCANS - 1):
                            decays(i, SCANS * p + k + 1, 1 - k % 2)
                        if experts and k < SETS:
                            high_part(i - 1, *two_on(p, k))

                with act.Fori(0, ROUNDS - 1) as p:
                    one_round(p, False)
                one_round(ROUNDS - 1, True)

            def turn(i, end, old, nxt):
                t, n = i - 1, i + 1
                if old:
                    pair(t, *LAST_BUT_ONE)
                if end:
                    high_part(i, *SECOND)
                    square(i, mix_norm)
                    nc.scalar.preload_act_table_set("natural_log_exp_and_others")
                    read_variance(i, mix_norm, W)
                    rough_rstd(i, mix_norm)
                if old:
                    pair(t, *LAST)
                if end:
                    high_part(i, *FIRST)
                    act.wait_ge(mix_norm["done"], i + 1)
                    nc.scalar.activation(h1_hi[:], h1[:], ACT.Copy).then_inc(h1_hi_done, 1)
                if nxt:
                    read_x(n)
                if end:
                    act.wait_ge(logits_done, i + 1)
                    nc.scalar.activation(ex[:], W[0:NB, 0:2 * EXPERTS].rearrange("p (b e) -> p b e", b=2), ACT.Exp,
                                         scale=-1.0).then_inc(ex_done, 1)
                if nxt:
                    tanh_z(n)
                if old:
                    square(t, out_norm)
                if nxt:
                    tanh_conv(n)
                if end:
                    act.wait_ge(shared_gu, i + 1)
                    nc.scalar.activation(tanh_s[:], GU[0][:, 0:N], ACT.Tanh, scale=0.5).then_inc(shared_tanh, 1)
                if old:
                    read_variance(t, out_norm, O)
                if nxt:
                    softplus_exp(n)
                if end:
                    gate_tanh(i, *FIRST)
                nc.scalar.preload_act_table_set("natural_log_exp_and_others")
                if nxt:
                    softplus_ln(n)
                if old:
                    rough_rstd(t, out_norm)
                if end:
                    high_part(i, 0, 0)
                    gate_tanh(i, *SECOND)
                    copy_weights(i, *FIRST)
                if nxt:
                    act.wait_ge(delta_done, n + 1)
                    decays(n, 0, 0)
                if end:
                    copy_weights(i, *SECOND)
                    high_part(i, 0, 1)
                    nc.scalar.activation(h1_kept[:], h1[:], ACT.Copy).then_inc(h1_kept_done, 1)

            periods(act, scans, turn)

        @block.vector
        def _(dve):
            dve.sem_inc(decay_free, 2)
            dve.sem_inc(bc_free, 2)
            dve.sem_inc(gu_free, 2)
            dve.sem_inc(wb_free, 1)
            dve.sem_inc(weighted, SETS)

            def setup():
                made = [0]

                def made_in_turn(ins):
                    made[0] += 1
                    ins.then_inc(consts_dve, 1)
                    dve.wait_ge(consts_dve, made[0])

                nc.vector.memset(one_col[:], 1.0)
                nc.vector.memset(eps_col[:], EPS)
                nc.vector.memset(small_col[:], SMALL)
                made_in_turn(nc.vector.memset(averager[:], 1.0 / DM))
                dve.wait_ge(weights_in, 16 * len(LOADS))
                for part in range(3):
                    nc.vector.tensor_scalar(xw[:, :, part, :], xw_raw[:, :, 1:1 + ROWS], 0.5, None, ALU.mult)
                nc.vector.tensor_scalar(dtw[:], xw_raw[:, :, 0:1].broadcast_to([P, KI, P]), 0.5, None, ALU.mult)
                for m in range(KM):
                    nc.vector.tensor_scalar(posb[:, m, 0:1], posb[:, m, 0:1], clsb[:, m:m + 1], None, ALU.add)
                    nc.vector.tensor_scalar(posb[:, m, 1:TOKENS], posb[:, m, 1:TOKENS], tokb[:, m:m + 1], None, ALU.add)
                dve.wait_ge(aexp_done, 3)
                nc.vector.tensor_tensor(sharedw_lo[:], sharedw[:, 0:GCOLS], sharedw_hi[:].bitcast(F32), ALU.subtract)
                nc.vector.tensor_scalar(aneg[:].rearrange("p s c -> p c s"), aexp[:].rearrange("p (c s) -> p c s", c=KI),
                                        -1.0, None, ALU.mult)
                dve.wait_ge(consts_pool, CONSTS_POOL)
                for c in range(KI):
                    made_in_turn(nc.vector.tensor_scalar(diag_d[:, c, :], ident[:], dpar[:, c:c + 1], 0.5, ALU.mult, ALU.mult))
                nc.vector.tensor_scalar(rstd[:, 0:1], one_col[:], 1.0, None, ALU.mult).then_inc(setup_done, 1)

            setup()

            def split(no, step, bank, rows):
                base = SPLITS * no
                nc.vector.tensor_copy(rows[:], bank[0:SPLIT, 0:N]).then_inc(step, 1)
                dve.wait_ge(step, base + 1)
                nc.vector.tensor_tensor(rest[:], bank[0:SPLIT, 0:N], rows[:], ALU.subtract).then_inc(step, 1)
                dve.wait_ge(step, base + 2)
                nc.vector.tensor_copy(mid[:], rest[:]).then_inc(step, 1)
                dve.wait_ge(step, base + 3)
                nc.vector.tensor_copy(rows[ROWS:2 * ROWS, :], mid[ROWS:2 * ROWS, :])
                nc.vector.tensor_tensor(rows[2 * ROWS:SPLIT, :], rest[2 * ROWS:SPLIT, :], mid[2 * ROWS:SPLIT, :],
                                        ALU.subtract).then_inc(step, 1)

            def tokens(i):
                dve.wait_ge(tok_done, i + 1)
                for m in range(KM):
                    h0m = h0[:, m, :].rearrange("p (a t) -> p a t", a=TI)
                    nc.vector.tensor_tensor(
                        h0m[:, :, 1:TOKENS], BC[0][:, m * NP:(m + 1) * NP].rearrange("p (a t) -> p a t", a=TI),
                        posb[:, m:m + 1, 1:TOKENS].broadcast_to([P, TI, PATCHES]), ALU.add)
                    last = nc.vector.tensor_copy(h0m[:, :, 0:1], posb[:, m:m + 1, 0:1].broadcast_to([P, TI, 1]))
                last.then_inc(h0_done, 1)

            def convolve(i, b):
                for k in range(TAPS - 1):
                    for c in range(2 * b, 2 * b + 2):
                        if k == 0:
                            dve.wait_ge(xpad_done, KI * i + c + 1)
                            dve.wait_ge(tap_done, KI * i + c + 1)
                        else:
                            dve.wait_ge(conv_done, CONV_OPS * i + CONV_OPS // 2 * b + 2 * (k - 1) + c % 2 + 1)
                        convc = conv[:, c, :].rearrange("p (a t) -> p a t", a=TI)
                        nc.vector.scalar_tensor_tensor(convc, xpad[:, c, :, k:k + TOKENS], convw[:, c, k:k + 1],
                                                       convc, ALU.mult, ALU.add).then_inc(conv_done, 1)

            def silu_z(i):
                for b in range(2):
                    dve.wait_ge(z_tanh, 2 * i + b + 1)
                    nc.vector.scalar_tensor_tensor(z2[:, 2 * b:2 * b + 2, :], half_tanh_z[:, 2 * b:2 * b + 2, :], 1.0,
                                                   two((BC[0], Y[0])[b]), ALU.add, ALU.mult).then_inc(z2_done, 1)

            def silu_conv(i):
                for b in range(2):
                    dve.wait_ge(conv_tanh, 2 * i + b + 1)
                    nc.vector.scalar_tensor_tensor(x2[:, 2 * b:2 * b + 2, :], half_tanh[:, 2 * b:2 * b + 2, :], 1.0,
                                                   conv[:, 2 * b:2 * b + 2, :], ALU.add, ALU.mult).then_inc(x2_done, 1)

            def softplus_small(i):
                dve.wait_ge(soft_step, 3 * i + 2)
                nc.vector.tensor_scalar(small[:], soft[:], SMALL, None, ALU.min).then_inc(small_done, 1)

            def softplus_sum(i):
                dve.wait_ge(soft_step, 3 * i + 3)
                nc.vector.scalar_tensor_tensor(soft[:], soft[:], ln_small[:], delta[:], ALU.max,
                                               ALU.add).then_inc(softplus_step, 1)
                dve.wait_ge(softplus_step, i + 1)
                dve.wait_ge(product_done, i + 1)
                nc.vector.scalar_tensor_tensor(delta[:], soft[:], ln_small[:], small[:], ALU.subtract,
                                               ALU.add).then_inc(delta_done, 1)

            def delta_x(i):
                dve.wait_ge(delta_done, i + 1)
                nc.vector.scalar_tensor_tensor(du[:], x2[:], 0.5, delta[:], ALU.mult, ALU.mult).then_inc(du_done, 1)
                dve.wait_ge(du_done, i + 1)

            def shared_expert(t):
                dve.wait_ge(shared_tanh, t + 1)
                nc.vector.scalar_tensor_tensor(act_s[:], tanh_s[:], 1.0, GU[0][:, 0:N], ALU.add,
                                               ALU.mult).then_inc(shared_step, 1)
                dve.wait_ge(shared_step, 2 * t + 1)
                nc.vector.scalar_tensor_tensor(hid_s[:], act_s[:], 0.5, GU[1][:, 0:N], ALU.mult,
                                               ALU.mult).then_inc(shared_step, 1)

            def drives(i, s, q):
                dve.wait_ge(bc_done, STATES * i + s + 1)
                nc.vector.tensor_tensor(drive[q][:], du[:], BC[q][:, None, 0:N].broadcast_to([P, KI, N]),
                                        ALU.mult).then_inc(drive_done, 1)

            def scan(i, s, q):
                dve.wait_ge(decay_done, STATES * i + s + 1)
                dve.wait_ge(drive_done, STATES * i + s + 1)
                nc.vector.tensor_tensor_scan(state[q][:].rearrange("p c n -> p (c n)"),
                                             decay[q][:].rearrange("p a t -> p (a t)"),
                                             drive[q][:].rearrange("p c n -> p (c n)"), 0.0,
                                             ALU.mult, ALU.add).then_inc(decay_free, 1)

            def reads(i, p, k):
                s, q = SCANS * p + k, k % 2
                dve.wait_ge(decay_free, STATES * i + s + 3)
                if q == 0:
                    dve.wait_ge(sum_free, STATES // 2 * i + SCANS // 2 * p + k // 2 + 1)
                nc.vector.tensor_tensor(read[k][:], state[q][:], BC[q][:, None, N:2 * N].broadcast_to([P, KI, N]),
                                        ALU.mult).then_inc(bc_free, 1)

            def act_gate(t, p, k, j):
                dve.wait_ge(tanh_done, 2 * pair_index(t, p, k) + j + 1)
                nc.vector.scalar_tensor_tensor(act_g[:, j, :], tanh_g[:, j, :], 1.0, GU[j][:, 0:N], ALU.add,
                                               ALU.mult).then_inc(act_done, 1)

            def times_up(t, p, k, j):
                dve.wait_ge(act_done, 2 * pair_index(t, p, k) + j + 1)
                if j == 0:
                    dve.wait_ge(weighted, set_credit(t, p, k))
                nc.vector.tensor_tensor(hid[k][:, j, :], act_g[:, j, :], GU[j][:, N:2 * N], ALU.mult).then_inc(gu_free, 1)

            def hidden(t, p, k):
                for j in range(2):
                    act_gate(t, p, k, j)
                    times_up(t, p, k, j)

            def centre(no, sems, source, bank):
                dve.wait_ge(sems["mean"], no + 1)
                nc.vector.tensor_tensor(centred[:], source[:], bank[:, None, 0:N].broadcast_to([P, KM, N]),
                                        ALU.subtract).then_inc(sems["centred"], 1)

            def router(i):
                done = [0]

                def in_turn(ins):
                    done[0] += 1
                    ins.then_inc(route_step, 1)
                    dve.wait_ge(route_step, ROUTE * i + done[0])

                def gate():
                    dve.sem_inc(route_gate, 1)

                dve.wait_ge(ex_done, i + 1)
                in_turn(nc.vector.tensor_scalar(ex[:], ex[:], 1.0, None, ALU.add))
                in_turn(nc.vector.reciprocal(score[:], ex[:]))
                in_turn(nc.vector.tensor_reduce(gsum[:, :, 0:GROUPS],
                                                score[:].rearrange("p b (g e) -> p b g e", g=GROUPS), AX.X, ALU.add))
                for b in range(2):
                    gate()
                    in_turn(nc.vector.max(gtop[:, b, :], gsum[:, b, :]))
                in_turn(nc.vector.tensor_copy(glist[:, :, 0:TOPG], gtop[:, :, 0:TOPG]))
                for b in range(2):
                    gate()
                    in_turn(nc.vector.match_replace(gleft[:, b, :], glist[:, b, :], gsum[:, b, :], -1.0))
                in_turn(nc.vector.tensor_scalar(gmask[:], gleft[:, :, 0:GROUPS], -1.0, None, ALU.is_equal))
                in_turn(nc.vector.tensor_tensor(
                    masked[:].rearrange("p b (g e) -> p b g e", g=GROUPS), score[:].rearrange("p b (g e) -> p b g e", g=GROUPS),
                    gmask[:, :, :, None].broadcast_to([NB, 2, GROUPS, PER_GROUP]), ALU.mult))
                for b in range(2):
                    gate()
                    in_turn(nc.vector.max(etop[:, b, :], masked[:, b, :]))
                for b in range(2):
                    gate()
                    in_turn(nc.vector.match_replace(eleft[:, b, :], etop[:, b, :], masked[:, b, :], -1.0))
                in_turn(nc.vector.scalar_tensor_tensor(wsel[:], eleft[:], -1.0, masked[:], ALU.is_equal, ALU.mult))
                in_turn(nc.vector.tensor_reduce(wsum[:], wsel[:], AX.X, ALU.add))
                in_turn(nc.vector.tensor_scalar(wsum[:], wsum[:], 1e-12, None, ALU.max))
                in_turn(nc.vector.reciprocal(winv[:], wsum[:]))
                for b in range(2):
                    last = nc.vector.tensor_scalar(w3[:, b], wsel[:, b:b + 1, :].broadcast_to([NB, 3, EXPERTS]),
                                                   winv[:, b:b + 1], 0.5, ALU.mult, ALU.mult)
                last.then_inc(route_step, 1)
                assert done[0] + 1 == ROUTE, done

            def scans(i, mixer, experts):
                t = i - 1

                def one_round(p, final):
                    for k in range(SCANS):
                        pair, more = experts and k < SETS, mixer and not (final and k == SCANS - 1)
                        if pair:
                            act_gate(t, p, k, 0)
                        if mixer:
                            reads(i, p, k)
                        if pair:
                            times_up(t, p, k, 0)
                            act_gate(t, p, k, 1)
                        if more:
                            drives(i, SCANS * p + k + 1, 1 - k % 2)
                        if pair:
                            times_up(t, p, k, 1)
                        if more:
                            scan(i, SCANS * p + k + 1, 1 - k % 2)

                with dve.Fori(0, ROUNDS - 1) as p:
                    one_round(p, False)
                one_round(ROUNDS - 1, True)

            def turn(i, end, old, nxt):
                t, n = i - 1, i + 1
                if old:
                    hidden(t, *LAST_BUT_ONE)
                if end:
                    dve.wait_ge(sum_free, STATES // 2 * (i + 1) + 2)
                    for b in range(2):
                        nc.vector.scalar_tensor_tensor(gated[:, 2 * b:2 * b + 2, :], two(Y[b]), 0.5,
                                                       z2[:, 2 * b:2 * b + 2, :], ALU.mult, ALU.mult).then_inc(gated_done, 1)
                    dve.wait_ge(outproj_done, i + 1)
                    nc.vector.tensor_tensor(r1[:], two(Y[0]), h0[:], ALU.add).then_inc(mix_norm["sum"], 1)
                    centre(i, mix_norm, r1, W)
                if nxt:
                    tokens(n)
                if end:
                    normalise(dve, nc.vector, i, mix_norm, h1)
                if old:
                    hidden(t, *LAST)
                if nxt:
                    convolve(n, 0)
                if old:
                    dve.wait_ge(hidw_free, PAIRS * (t + 1) + SETS)
                    dve.wait_ge(h1_kept_done, t + 1)
                    nc.vector.tensor_tensor(r2[:], two(O), h1_kept[:], ALU.add).then_inc(out_norm["sum"], 1)
                if nxt:
                    convolve(n, 1)
                if old:
                    dve.wait_ge(out_norm["sum"], t + 1)
                    centre(t, out_norm, r2, O)
                if nxt:
                    silu_z(n)
                    silu_conv(n)
                if end:
                    shared_expert(i)
                    router(i)
                if nxt:
                    softplus_small(n)
                    dve.wait_ge(rows_done, n + 1)
                    split(n, bc_split, BC[1], bc_rows)
                if end:
                    hidden(i, *FIRST)
                    dve.wait_ge(w3_turned, i + 1)
                    split(i, w_split, W, w_rows)
                if nxt:
                    softplus_sum(n)
                if end:
                    hidden(i, *SECOND)
                if nxt:
                    delta_x(n)
                    drives(n, 0, 0)
                    scan(n, 0, 0)

            periods(dve, scans, turn)


def kernel(**inputs):
    import numpy as _np
    import concourse.bacc as _bacc
    from concourse import mybir as _mybir
    from concourse.bass_utils import run_bass_kernel_spmd as _run

    a = {k: _np.asarray(v) for k, v in inputs.items()}

    def rows(w):
        w = w.reshape(w.shape[0] // P, P, *w.shape[1:])
        return w.transpose(1, 0, *range(2, w.ndim))

    x = _np.zeros((TILES * TI, CHANNELS, GRID, PATCH, GRID, PATCH), a["x"].dtype)
    x[:IMAGES] = a["x"].reshape(IMAGES, CHANNELS, GRID, PATCH, GRID, PATCH)
    x = x.reshape(TILES, TI, CHANNELS, GRID, PATCH, GRID, PATCH).transpose(0, 2, 4, 6, 1, 3, 5)
    x = x.reshape(TILES, KF, P, NP).transpose(0, 2, 1, 3)

    def expert(gate, up, down):
        e = gate.shape[0]
        g, u = (w.transpose(0, 2, 1).reshape(e, KM, P, HID).transpose(0, 2, 1, 3).reshape(e, P, KM * HID)
                for w in (gate, up))
        return _np.concatenate([g, u, down.transpose(0, 2, 1)], axis=2)

    experts = expert(a["L0_ffn_expert_gate"], a["L0_ffn_expert_up"], a["L0_ffn_expert_down"])
    experts = experts.reshape(PAIRS, 2, P, WCOLS).transpose(0, 2, 1, 3)

    given = {
        "x": x,
        "w_tok": rows(a["L0_tok_W"].T),
        "b_tok": rows(a["L0_tok_b"]),
        "cls_tok": rows(a["L0_tok_cls_token"].reshape(DM)),
        "pos": rows(a["L0_tok_pos_enc"][0].T),
        "w_in": rows(a["L0_attn_W_in"].T),
        "conv_w": rows(a["L0_attn_conv_w"][:, 0, :]),
        "conv_b": rows(a["L0_attn_conv_b"]),
        "w_x": rows(a["L0_attn_W_x"].T),
        "w_dt": rows(a["L0_attn_W_dt"][:, 0]),
        "b_dt": rows(a["L0_attn_b_dt"]),
        "a_log": rows(a["L0_attn_A_log"]).reshape(P, KI * STATES),
        "d_par": rows(a["L0_attn_D_param"]),
        "w_out": rows(a["L0_attn_W_out"].T),
        "gate_w": rows(a["L0_ffn_gate_w"].T),
        "experts_gu": experts[..., 0:GCOLS],
        "experts_down": experts[..., GCOLS:WCOLS],
        "shared": expert(*(a[f"L0_ffn_shared_{n}_w"][None] for n in ("gate", "up", "down")))[0],
    }
    nc = _bacc.Bacc("TRN2", target_bir_lowering=False, num_devices=1)
    arrays, args = {}, []
    for name, v in given.items():
        v = _np.ascontiguousarray(v)
        arrays[f"in_{name}_dram"] = v
        args.append(nc.dram_tensor(f"in_{name}_dram", v.shape, _mybir.dt.from_np(v.dtype), kind="ExternalInput").ap())
    args.append(nc.dram_tensor("out_dram", (TILES, P, KM, N), _mybir.dt.float32, kind="ExternalOutput").ap())
    build(nc, *args)
    r = _run(nc, [arrays], core_ids=[0])
    got = r.results[0]["out_dram"].reshape(TILES, P, KM, TI, TOKENS).transpose(0, 3, 4, 2, 1)
    return _np.ascontiguousarray(got.reshape(TILES * TI, TOKENS, DM)[:IMAGES])
```

```python
from contextlib import ExitStack

import concourse.bass as bass
from concourse import mybir

F32 = mybir.dt.float32
BF16 = mybir.dt.bfloat16
ALU = mybir.AluOpType
ACT = mybir.ActivationFunctionType
AX = mybir.AxisListType

P = 128
IMAGES, CHANNELS, SIDE, PATCH = 64, 3, 96, 16
GRID = SIDE // PATCH
PATCHES = GRID * GRID
TOKENS = PATCHES + 1
FEATS = CHANNELS * PATCH * PATCH
DM, DI, STATES, TAPS = 256, 512, 16, 4
EXPERTS, TOPK, GROUPS, TOPG, HID = 32, 8, 8, 4, 128
PER_GROUP = EXPERTS // GROUPS
TI = 6
TILES = -(-IMAGES // TI)
N = TI * TOKENS
NP = TI * PATCHES
KF, KM, KI = FEATS // P, DM // P, DI // P
FIRST_IMAGES = IMAGES - (TILES - 1) * TI
PADT = TOKENS + TAPS - 1
ROWS = 2 * STATES
SPLIT = 3 * ROWS
GCOLS = 4 * P
WCOLS = GCOLS + DM
PAIRS = EXPERTS // 2
EARLY = 2
ROUNDS = 4
SETS = 3
SCANS = STATES // ROUNDS
POOL_READ = 1
AHEAD_BC = [(3,), (4,), (5, 6)]
AHEAD_DECAY = [(2, 3), (4,), (5,)]
FIRST, SECOND, LAST_BUT_ONE, LAST = (-1, 1), (-1, 2), (ROUNDS, 0), (ROUNDS, 1)


def pair_no(p, k):
    return EARLY + SETS * p + k


RESIDENT = [FIRST, SECOND, LAST_BUT_ONE, LAST]


def is_resident(p, k):
    return isinstance(p, int) and (p, k) in RESIDENT


def weight_set(p, k):
    return SETS + RESIDENT.index((p, k)) if is_resident(p, k) else k


def loads(t, p, k):
    return 1 if is_resident(p, k) else ROUNDS * t + p + 1


def images(t):
    return FIRST_IMAGES if isinstance(t, int) and t == 0 else TI


def width(t):
    return TOKENS * images(t)


def half(t):
    return width(t) // 2


def chunks(t, buffer, size=TOKENS):
    n = buffer.shape[1] // TI // size
    return buffer[:, 0:n * size * images(t)].rearrange("p (c n) -> p c n", c=n)


EPS = 1e-5
SMALL = 2.0 ** -11


def build(nc, x, w_tok, b_tok, cls_tok, pos, w_in, conv_w, conv_b, w_x, w_dt, b_dt, a_log, d_par, w_out,
          gate_w, experts, shared, out):
    with ExitStack() as ctx:
        def sb(name, shape, dt=F32):
            return ctx.enter_context(nc.sbuf_tensor(name, shape, dt))

        def ps(name):
            return ctx.enter_context(nc.psum_tensor(name, [P, 512], F32))

        def sem(name):
            return ctx.enter_context(nc.semaphore(name))

        tokw = sb("tokw", [P, KF, DM])
        inw = sb("inw", [P, KM, 2 * DI])
        outw = sb("outw", [P, KI, DM])
        gatew = sb("gatew", [P, KM, EXPERTS])
        sharedw = sb("sharedw", [P, WCOLS])
        xw_raw = sb("xw_raw", [P, KI, 1 + ROWS])
        xw = sb("xw", [P, KI, 3, ROWS])
        dtw = sb("dtw", [P, KI, P])
        posb = sb("posb", [P, KM, TOKENS])
        tokb = sb("tokb", [P, KM])
        clsb = sb("clsb", [P, KM])
        convw = sb("convw", [P, KI, TAPS])
        convb = sb("convb", [P, KI])
        dt_scale = sb("dt_scale", [P, KI])
        dt_bias = sb("dt_bias", [P, KI])
        alog = sb("alog", [P, KI * STATES])
        aexp = sb("aexp", [P, KI * STATES])
        aneg = sb("aneg", [P, STATES, KI])
        dpar = sb("dpar", [P, KI])
        ident = sb("ident", [P, P])
        half_d = sb("half_d", [P, KI])
        averager = sb("averager", [P, P])
        sel = sb("sel", [SPLIT, ROWS, P], BF16)
        one_col = sb("one_col", [P, 1])
        eps_col = sb("eps_col", [P, 1])
        small_col = sb("small_col", [P, 1])
        ln_small = sb("ln_small", [P, 1])

        patches = sb("patches", [P, KF * NP])
        h0 = sb("h0", [P, KM * N])
        xpad = sb("xpad", [P, KI, TI, PADT])
        half_tanh_z = sb("half_tanh_z", [P, KI * N])
        x2 = sb("x2", [P, KI * N])
        z2 = sb("z2", [P, KI * N])
        delta = sb("delta", [P, KI * N])
        du = sb("du", [P, KI * N])
        bc_rows = sb("bc_rows", [SPLIT, N], BF16)
        w_rows = sb("w_rows", [SPLIT, N], BF16)
        rest = sb("rest", [SPLIT, N])
        mid = sb("mid", [SPLIT, N], BF16)
        decay = [sb(f"decay{k}", [P, KI * N]) for k in range(SCANS)]
        drive = [sb(f"drive{q}", [P, KI * N]) for q in range(2)]
        state = [sb(f"state{q}", [P, KI * N]) for q in range(SCANS)]
        spread_bc = [sb(f"spread_bc{k}", [P, 2 * N]) for k in range(SCANS)]
        y = sb("y", [P, KI * N])
        read = [sb(f"read{q}", [P, KI * N]) for q in range(SCANS)]
        conv, half_tanh = read[0], read[2]
        soft, small, series = state[3], drive[1], read[1]
        gated = x2
        r1 = sb("r1", [P, KM * N])
        r2 = r1
        centred = sb("centred", [P, KM * N])
        squared = sb("squared", [P, KM * N])
        var_eps = sb("var_eps", [P, N])
        rough = sb("rough", [P, N])
        newton = sb("newton", [P, 2 * N])
        rstd = sb("rstd", [P, N])
        h1 = sb("h1", [P, KM * N])
        h1_kept = sb("h1_kept", [P, KM * N])
        outb = sb("outb", [P, KM * N])

        ex = sb("ex", [N // 2, 2, EXPERTS])
        score = sb("score", [N // 2, 2, EXPERTS])
        gsum = sb("gsum", [N // 2, 2, GROUPS + 8 - TOPG])
        gtop = sb("gtop", [N // 2, 2, 8])
        glist = sb("glist", [N // 2, 2, 8])
        gleft = sb("gleft", [N // 2, 2, GROUPS + 8 - TOPG])
        gmask = sb("gmask", [N // 2, 2, GROUPS])
        masked = sb("masked", [N // 2, 2, EXPERTS])
        etop = sb("etop", [N // 2, 2, 8])
        eleft = sb("eleft", [N // 2, 2, EXPERTS])
        wsel = sb("wsel", [N // 2, 2, EXPERTS])
        wsum = sb("wsum", [N // 2, 2])
        winv = sb("winv", [N // 2, 2])
        w3 = sb("w3", [N // 2, 2, 3, EXPERTS])

        expertw = [sb(f"expertw{k}", [P, 2, WCOLS]) for k in range(SETS + len(RESIDENT))]
        tanh_g = sb("tanh_g", [P, 2 * N])
        act_g = sb("act_g", [P, 2 * N])
        hid = [sb(f"hid{k}", [P, 2 * N]) for k in range(SETS)]
        spread_w = [sb(f"spread_w{k}", [P, 2 * N]) for k in range(SETS)]
        hidw = [sb(f"hidw{k}", [P, 2 * N]) for k in range(SETS)]
        tanh_s = sb("tanh_s", [P, N])
        act_s = sb("act_s", [P, N])
        hid_s = sb("hid_s", [P, N])

        Y = [ps("Y0"), ps("Y1")]
        GU = [ps("GU0"), ps("GU1")]
        BC = [ps("BC0"), ps("BC1")]
        O = ps("O")
        W = ps("W")

        X_BANKS, Z_BANKS = (Y[1], BC[1]), (Y[0], Y[1])

        def two(t, bank):
            return bank[:, 0:2 * width(t)].rearrange("p (c n) -> p c n", c=2)

        tokw_in = sem("tokw_in")
        embed_in = sem("embed_in")
        mixer_in = sem("mixer_in")
        later_in = sem("later_in")
        ident_step = sem("ident_step")
        cleared = sem("cleared")
        sel_step = sem("sel_step")
        aexp_done = sem("aexp_done")
        columns_done = sem("columns_done")
        posb_step = sem("posb_step")
        mixer_setup = sem("mixer_setup")
        patches_in = sem("patches_in")
        tok_done = sem("tok_done")
        h0_done = sem("h0_done")
        xz_done = sem("xz_done")
        xpad_done = sem("xpad_done")
        tap_done = sem("tap_done")
        conv_done = sem("conv_done")
        conv_tanh = sem("conv_tanh")
        z_tanh = sem("z_tanh")
        x2_done = sem("x2_done")
        z2_done = sem("z2_done")
        dt_done = sem("dt_done")
        rows_done = sem("rows_done")
        bc_split = sem("bc_split")
        w_split = sem("w_split")
        soft_step = sem("soft_step")
        small_done = sem("small_done")
        series_done = sem("series_done")
        product_done = sem("product_done")
        softplus_step = sem("softplus_step")
        delta_done = sem("delta_done")
        du_done = sem("du_done")
        y_init = sem("y_init")
        bc_done = sem("bc_done")
        decay_done = sem("decay_done")
        drive_done = sem("drive_done")
        decay_free = sem("decay_free")
        bc_copied = sem("bc_copied")
        read_done = sem("read_done")
        pool_read = sem("pool_read")
        y_added = sem("y_added")
        gated_done = sem("gated_done")
        outproj_done = sem("outproj_done")
        def norm_sems(of):
            return {n: sem(f"{of}_{n}") for n in ("sum", "mean", "centred", "squared", "var", "eps", "rough", "newton", "gate", "done")}

        mix_norm = norm_sems("mix_norm")
        out_norm = norm_sems("out_norm")
        logits_done = sem("logits_done")
        ex_done = sem("ex_done")
        route_step = sem("route_step")
        route_gate = sem("route_gate")
        w3_turned = sem("w3_turned")
        shared_gu = sem("shared_gu")
        shared_tanh = sem("shared_tanh")
        shared_step = sem("shared_step")
        shared_down = sem("shared_down")
        h1_kept_done = sem("h1_kept_done")
        expertw_in = [sem(f"expertw_in{k}") for k in range(SETS + len(RESIDENT))]
        gu_done = sem("gu_done")
        tanh_done = sem("tanh_done")
        act_done = sem("act_done")
        gu_free = sem("gu_free")
        wb_done = sem("wb_done")
        wb_free = sem("wb_free")
        weighted = sem("weighted")
        hidw_free = sem("hidw_free")
        out_sent = sem("out_sent")

        EMBED_LOADS = [(posb, pos), (tokb, b_tok), (clsb, cls_tok)]
        MIXER_LOADS = [(inw, w_in), (convw, conv_w), (convb, conv_b), (alog, a_log), (xw_raw, w_x), (dpar, d_par),
                       (dt_scale, w_dt), (dt_bias, b_dt)]
        LATER_LOADS = [(sharedw, shared), (outw, w_out), (gatew, gate_w)]
        CLEARED, SEL_STEPS = 3 + SCANS, 4
        CONV_OPS = KI * (TAPS - 1)
        SPLITS = 4
        ROUTE = 19

        def periods(eng, scans, turn):
            turn(-1, False, False, True)
            scans(0, True, False)
            turn(0, True, False, True)
            scans(1, True, True)
            turn(1, True, True, True)
            with eng.Fori(2, TILES - 1) as i:
                scans(i, True, True)
                turn(i, True, True, True)
            scans(TILES - 1, True, True)
            turn(TILES - 1, True, True, False)
            scans(TILES, False, True)
            turn(TILES, False, True, False)

        def pair_index(t, p, k):
            return PAIRS * t + pair_no(p, k)

        def set_credit(t, p, k):
            return pair_index(t, p, k) + (SETS if isinstance(p, int) and (p, k) == FIRST else 1)

        def normalise(eng, ops, no, sems, to):
            eng.wait_ge(sems["rough"], 2 * no + 2)
            ops.tensor_tensor(chunks(no, newton)[:, 0, :], var_eps[:, 0:width(no)], rough[:, 0:width(no)], ALU.mult).then_inc(sems["newton"], 1)
            eng.wait_ge(sems["newton"], 4 * no + 1)
            ops.tensor_tensor(chunks(no, newton)[:, 1, :], chunks(no, newton)[:, 0, :], rough[:, 0:width(no)], ALU.mult).then_inc(sems["newton"], 1)
            eng.wait_ge(sems["newton"], 4 * no + 2)
            eng.sem_inc(sems["gate"], 1)
            ops.tensor_scalar(chunks(no, newton)[:, 0, :], chunks(no, newton)[:, 1, :], -0.5, 1.5, ALU.mult, ALU.add).then_inc(sems["newton"], 1)
            eng.wait_ge(sems["newton"], 4 * no + 3)
            ops.tensor_tensor(rstd[:, 0:width(no)], chunks(no, newton)[:, 0, :], rough[:, 0:width(no)], ALU.mult).then_inc(sems["newton"], 1)
            eng.wait_ge(sems["newton"], 4 * no + 4)
            ops.tensor_tensor(chunks(no, to), chunks(no, centred), rstd[:, None, 0:width(no)].broadcast_to([P, KM, width(no)]),
                              ALU.mult).then_inc(sems["done"], 1)

        def dve_reads(i, p, k):
            return (SCANS - 1) * (ROUNDS * i + p) + k + (1 if k < POOL_READ else 0)

        block = ctx.enter_context(nc.Block())

        @block.sync
        def _(sp):
            sp.sem_inc(out_sent, 16)
            sp.dma_start(tokw[:], w_tok).then_inc(tokw_in, 16)
            sp.dma_start(chunks(0, patches, PATCHES), x[0][:, :, 0:PATCHES * images(0)]).then_inc(patches_in, 16)
            for loads, loaded in ((EMBED_LOADS, embed_in), (MIXER_LOADS, mixer_in), (LATER_LOADS, later_in)):
                for to, of in loads:
                    sp.dma_start(to[:], of).then_inc(loaded, 16)

            def load_weights(t, p, k):
                if not isinstance(p, int) or p > 0:
                    sp.wait_ge(hidw_free, set_credit(t, p, k))
                elif not isinstance(t, int) or t > 0:
                    sp.wait_ge(hidw_free, pair_index(t - 1, ROUNDS - 1, k) + 1 + SETS)
                sp.dma_start(expertw[k][:], experts[pair_no(p, k)]).then_inc(expertw_in[k], 16)

            def load_patches(t):
                sp.wait_ge(tok_done, t)
                sp.dma_start(chunks(t, patches, PATCHES), x[t]).then_inc(patches_in, 16)

            def send(t):
                sp.wait_ge(out_norm["done"], t + 1)
                sp.dma_start(out[t][:, :, 0:width(t)], chunks(t, outb)).then_inc(out_sent, 16)

            def tile(t, first, more):
                for k in range(SETS):
                    load_weights(t, 0, k)
                if more:
                    load_patches(t + 2)
                with sp.Fori(1, ROUNDS) as p:
                    for k in range(SETS):
                        load_weights(t, p, k)
                if not first:
                    send(t - 1)

            load_patches(1)
            for p, k in RESIDENT:
                n = weight_set(p, k)
                sp.dma_start(expertw[n][:], experts[pair_no(p, k)]).then_inc(expertw_in[n], 16)
            tile(0, True, True)
            tile(1, False, True)
            with sp.Fori(2, TILES - 2) as t:
                tile(t, False, True)
            tile(TILES - 2, False, False)
            tile(TILES - 1, False, False)
            send(TILES - 1)
            sp.wait_ge(out_sent, 16 * (TILES + 1))

        @block.gpsimd
        def _(pool):
            nc.gpsimd.memset(ident[:], 0.0).then_inc(ident_step, 1)
            pool.wait_ge(ident_step, 1)
            nc.gpsimd.affine_select(out=ident[:], in_=ident[:], compare_op=ALU.not_equal, fill=1.0, base=0,
                                    pattern=[[-1, P]], channel_multiplier=1).then_inc(ident_step, 1)
            nc.gpsimd.memset(xpad[:], 0.0).then_inc(cleared, 1)
            for k in range(SCANS):
                nc.gpsimd.memset(decay[k][:], 0.0).then_inc(cleared, 1)
            nc.gpsimd.memset(glist[:], -2.0).then_inc(cleared, 1)
            nc.gpsimd.memset(gsum[:], -2.0).then_inc(cleared, 1)
            nc.gpsimd.memset(sel[:], 0.0).then_inc(sel_step, 1)
            for part in range(3):
                pool.wait_ge(sel_step, 1 + part)
                nc.gpsimd.affine_select(out=sel[:], in_=sel[:], compare_op=ALU.not_equal, fill=1.0,
                                        base=-ROWS * part, pattern=[[-1, ROWS], [0, P]],
                                        channel_multiplier=1).then_inc(sel_step, 1)
            pool.sem_inc(y_added, SCANS)

            def weight(t, p, k):
                g = pair_index(t, p, k)
                pool.wait_ge(gu_free, 2 * g + 4)
                pool.wait_ge(wb_free, g + 2)
                pool.wait_ge(hidw_free, set_credit(t, p, k))
                nc.gpsimd.tensor_tensor(chunks(t, hidw[k]), chunks(t, hid[k]), chunks(t, spread_w[k]), ALU.mult).then_inc(weighted, 1)

            def reads(i, p, k):
                pool.wait_ge(decay_free, STATES * i + SCANS * p + k + 1 + SCANS)
                pool.wait_ge(bc_copied, STATES * i + SCANS * p + k + 3)
                nc.gpsimd.tensor_tensor(
                    chunks(i, read[k]), chunks(i, state[k]),
                    spread_bc[k][:, None, width(i):2 * width(i)].broadcast_to([P, KI, width(i)]),
                    ALU.mult).then_inc(pool_read, 1)

            def add_up(i, p, k):
                if k == POOL_READ:
                    pool.wait_ge(pool_read, ROUNDS * i + p + 1)
                else:
                    pool.wait_ge(read_done, dve_reads(i, p, k))
                pool.wait_ge(y_added, STATES * i + SCANS * p + k + SCANS)
                if k == 0:
                    pool.wait_ge(y_init, i + 1)
                nc.gpsimd.tensor_tensor(chunks(i, y), chunks(i, y), chunks(i, read[k]), ALU.add).then_inc(y_added, 1)

            def scans(i, mixer, experts):
                with pool.Fori(0, ROUNDS) as p:
                    for k in range(SETS):
                        if mixer:
                            if k == POOL_READ:
                                reads(i, p, k)
                            add_up(i, p, k)
                        if experts:
                            weight(i - 1, p, k)
                    if mixer:
                        add_up(i, p, SCANS - 1)

            def turn(i, end, old, nxt):
                t, n = i - 1, i + 1
                if old:
                    weight(t, *LAST_BUT_ONE)
                    weight(t, *LAST)
                if nxt:
                    pool.wait_ge(series_done, n + 1)
                    nc.gpsimd.tensor_tensor(chunks(n, small), chunks(n, small), chunks(n, series), ALU.mult).then_inc(product_done, 1)
                if old and end:
                    pool.wait_ge(out_sent, 16 * (t + 1))
                    normalise(pool, nc.gpsimd, t, out_norm, outb)
                if end:
                    weight(i, *FIRST)
                    weight(i, *SECOND)

            periods(pool, scans, turn)

        @block.tensor
        def _(pe):
            pe.sem_inc(hidw_free, SETS)
            pe.wait_ge(tokw_in, 16)

            def project_patches(i, m):
                pe.wait_ge(patches_in, 16 * (i + 1))
                for k in range(KF):
                    mm = nc.tensor.matmul(BC[0][:, m * PATCHES * images(i):(m + 1) * PATCHES * images(i)], tokw[:, k, m * P:(m + 1) * P],
                                          chunks(i, patches, PATCHES)[:, k, :], start=(k == 0), stop=(k == KF - 1))
                if m == KM - 1:
                    mm.then_inc(tok_done, 1)


            def project_in(i, b, banks, first_chunk):
                for c in range(2):
                    for k in range(KM):
                        at = first_chunk + 2 * b + c
                        mm = nc.tensor.matmul(banks[b][:, c * width(i):(c + 1) * width(i)], inw[:, k, at * P:(at + 1) * P],
                                              chunks(i, h0)[:, k, :], start=(k == 0), stop=(k == KM - 1))
                mm.then_inc(xz_done, 1)

            def project_x(i):
                pe.wait_ge(x2_done, 2 * i + 2)
                for c in range(KI):
                    mm = nc.tensor.matmul(BC[0][:, 0:width(i)], dtw[:, c, :], chunks(i, x2)[:, c, :], start=(c == 0), stop=(c == KI - 1))
                mm.then_inc(dt_done, 1)
                for c in range(KI):
                    mm = nc.tensor.matmul(BC[1][0:SPLIT, 0:width(i)], xw[:, c].rearrange("p a b -> p (a b)"), chunks(i, x2)[:, c, :],
                                          start=(c == 0), stop=(c == KI - 1))
                mm.then_inc(rows_done, 1)

            def products(t, bank, at, w, tokens):
                for k in range(KM):
                    mm = nc.tensor.matmul(bank[:, at:at + width(t)], w[:, k * P:(k + 1) * P], chunks(t, tokens)[:, k, :],
                                          start=(k == 0), stop=(k == KM - 1))
                return mm

            def shared_gate_up(t):
                for g in range(2):
                    mm = products(t, GU[g], 0, sharedw[:, 2 * g * P:], h1)
                mm.then_inc(shared_gu, 1)

            def shared_out(t):
                pe.wait_ge(shared_step, 2 * t + 2)
                for m in range(KM):
                    mm = nc.tensor.matmul(O[:, m * width(t):(m + 1) * width(t)], sharedw[:, (4 + m) * P:(5 + m) * P], hid_s[:, 0:width(t)],
                                          start=(m == 0), stop=False, skip_group_check=True)

            def spread(i, p, k):
                s, q = SCANS * p + k, k % 2
                pe.wait_ge(bc_copied, STATES * i + s + 1)
                for j in range(2):
                    mm = nc.tensor.matmul(BC[q][:, j * width(i):(j + 1) * width(i)], sel[:, STATES * j + s, :],
                                          bc_rows[:, 0:width(i)], start=True, stop=True)
                mm.then_inc(bc_done, 1)

            def gate_up(t, p, k):
                n = weight_set(p, k)
                pe.wait_ge(expertw_in[n], 16 * loads(t, p, k))
                for j in range(2):
                    pe.wait_ge(gu_free, 2 * pair_index(t, p, k) + j + 1)
                    for g in range(2):
                        mm = products(t, GU[j], g * width(t), expertw[n][:, j, 2 * g * P:],
                                      h1 if isinstance(p, int) and p < 0 else h1_kept)
                    mm.then_inc(gu_done, 1)

            def spread_weights(t, p, k):
                pe.wait_ge(wb_free, pair_index(t, p, k) + 1)
                for j in range(2):
                    mm = nc.tensor.matmul(W[:, j * width(t):(j + 1) * width(t)], sel[:, 2 * pair_no(p, k) + j, :], w_rows[:, 0:width(t)],
                                          start=True, stop=True)
                mm.then_inc(wb_done, 1)

            def down(t, p, k):
                pe.wait_ge(weighted, pair_index(t, p, k) + SETS + 1)
                for j in range(2):
                    for c in range(KM):
                        mm = nc.tensor.matmul(O[:, c * width(t):(c + 1) * width(t)], expertw[weight_set(p, k)][:, j, GCOLS + c * P:GCOLS + (c + 1) * P],
                                              chunks(t, hidw[k])[:, j, :], start=False, stop=False, skip_group_check=True)
                mm.then_inc(hidw_free, 1)

            def mean(no, sems, source, bank):
                pe.wait_ge(sems["sum"], no + 1)
                for k in range(KM):
                    mm = nc.tensor.matmul(bank[:, 0:width(no)], averager[:], chunks(no, source)[:, k, :], start=(k == 0), stop=(k == KM - 1))
                mm.then_inc(sems["mean"], 1)

            def variance(no, sems, bank):
                pe.wait_ge(sems["squared"], no + 1)
                for k in range(KM):
                    mm = nc.tensor.matmul(bank[:, 0:width(no)], averager[:], chunks(no, squared)[:, k, :], start=(k == 0), stop=(k == KM - 1))
                mm.then_inc(sems["var"], 1)

            def project_out(i):
                pe.wait_ge(gated_done, 2 * i + 2)
                for m in range(KM):
                    for c in range(KI):
                        mm = nc.tensor.matmul(Y[0][:, m * width(i):(m + 1) * width(i)], outw[:, c, m * P:(m + 1) * P],
                                              chunks(i, gated)[:, c, :], start=(c == 0), stop=(c == KI - 1))
                mm.then_inc(outproj_done, 1)

            def logits(i):
                pe.wait_ge(mix_norm["done"], i + 1)
                for b in range(2):
                    for k in range(KM):
                        mm = nc.tensor.matmul(W[0:half(i), b * EXPERTS:(b + 1) * EXPERTS], chunks(i, h1)[:, k, b * half(i):(b + 1) * half(i)],
                                              gatew[:, k, :], start=(k == 0), stop=(k == KM - 1))
                mm.then_inc(logits_done, 1)

            def turn_weights(i):
                pe.wait_ge(route_step, ROUTE * (i + 1))
                for b in range(2):
                    mm = nc.tensor.transpose(W[0:SPLIT, b * half(i):(b + 1) * half(i)],
                                             w3[0:half(i), b].rearrange("p a e -> p (a e)"), ident[0:half(i), 0:half(i)])
                mm.then_inc(w3_turned, 1)

            def scans(i, mixer, experts):
                t = i - 1

                def one_round(p, first, final):
                    for k in range(SETS):
                        if experts:
                            gate_up(t, p, k)
                            if first and k == 0:
                                down(t, *FIRST)
                            spread_weights(t, p, k)
                        for ahead in AHEAD_BC[k]:
                            if mixer and not (final and ahead >= SCANS):
                                spread(i, p, ahead)
                        if experts:
                            down(t, *((p, k - 1) if k else SECOND if first else (p - 1, 2)))

                if experts:
                    pe.wait_ge(h1_kept_done, t + 1)
                one_round(0, True, False)
                with pe.Fori(1, ROUNDS - 1) as p:
                    one_round(p, False, False)
                one_round(ROUNDS - 1, False, True)

            def turn(i, end, old, nxt):
                t, n = i - 1, i + 1
                if old:
                    gate_up(t, *LAST_BUT_ONE)
                    spread_weights(t, *LAST_BUT_ONE)
                    down(t, ROUNDS - 1, 2)
                if end:
                    pe.wait_ge(bc_copied, STATES * (i + 1) + 2)
                if nxt:
                    project_patches(n, 0)
                if end:
                    project_out(i)
                if old and end:
                    down(t, *LAST_BUT_ONE)
                if end:
                    if old:
                        pe.wait_ge(wb_free, pair_index(t, *LAST_BUT_ONE) + 2)
                    mean(i, mix_norm, r1, W)
                if nxt:
                    project_patches(n, 1)
                if end:
                    variance(i, mix_norm, W)
                if old:
                    gate_up(t, *LAST)
                    if end:
                        pe.wait_ge(mix_norm["eps"], i + 1)
                    if not end:
                        down(t, *LAST_BUT_ONE)
                    spread_weights(t, *LAST)
                if nxt:
                    if not end:
                        pe.wait_ge(mixer_in, 16 * len(MIXER_LOADS))
                    pe.wait_ge(h0_done, n + 1)
                    for b in range(2):
                        project_in(n, b, X_BANKS, 0)
                if end:
                    if old:
                        pe.wait_ge(wb_free, pair_index(t, *LAST) + 2)
                    logits(i)
                if old:
                    down(t, *LAST)
                if end:
                    shared_gate_up(i)
                if old:
                    mean(t, out_norm, r2, O)
                if nxt:
                    project_in(n, 0, Z_BANKS, KI)
                    if not end:
                        pe.wait_ge(mixer_setup, 1)
                        pe.wait_ge(sel_step, SEL_STEPS)
                    project_x(n)
                if old:
                    variance(t, out_norm, O)
                if end:
                    pe.wait_ge(shared_step, 2 * i + 2)
                    gate_up(i, *FIRST)
                    turn_weights(i)
                    if old:
                        pe.wait_ge(out_norm["eps"], t + 1)
                    shared_out(i)
                if end:
                    gate_up(i, *SECOND)
                    pe.wait_ge(w_split, SPLITS * (i + 1))
                    spread_weights(i, *FIRST)
                if nxt:
                    pe.wait_ge(bc_split, SPLITS * (n + 1))
                    pe.wait_ge(soft_step, 3 * n + 1)
                    spread(n, 0, 0)
                    spread(n, 0, 1)
                    project_in(n, 1, Z_BANKS, KI)
                    spread(n, 0, 2)
                    if not end:
                        pe.wait_ge(later_in, 16 * len(LATER_LOADS))
                if end:
                    spread_weights(i, *SECOND)

            periods(pe, scans, turn)

        @block.scalar
        def _(act):
            act.wait_ge(mixer_in, 16 * len(MIXER_LOADS))
            nc.scalar.activation(aexp[:], alog[:], ACT.Exp).then_inc(aexp_done, 1)
            act.wait_ge(columns_done, 1)
            nc.scalar.activation(ln_small[:], small_col[:], ACT.Ln, bias=one_col[:]).then_inc(aexp_done, 1)
            act.wait_ge(cleared, CLEARED)
            act.sem_inc(bc_copied, 2)


            def read_x(i):
                for b in range(2):
                    act.wait_ge(xz_done, 4 * i + b + 1)
                    for c in range(2 * b, 2 * b + 2):
                        src = X_BANKS[b][:, (c % 2) * width(i):(c % 2 + 1) * width(i)]
                        nc.scalar.activation(xpad[:, c, 0:images(i), TAPS - 1:PADT], src.rearrange("p (a t) -> p a t", a=images(i)),
                                             ACT.Copy).then_inc(xpad_done, 1)
                        nc.scalar.activation(chunks(i, conv)[:, c, :], src, ACT.Identity, scale=convw[:, c, TAPS - 1:TAPS],
                                             bias=convb[:, c:c + 1]).then_inc(tap_done, 1)

            def tanh_z(i):
                for b in range(2):
                    act.wait_ge(xz_done, 4 * i + 3 + b)
                    nc.scalar.activation(chunks(i, half_tanh_z)[:, 2 * b:2 * b + 2, :], two(i, Z_BANKS[b]), ACT.Tanh,
                                         scale=0.5).then_inc(z_tanh, 1)

            def tanh_conv(i):
                for b in range(2):
                    act.wait_ge(conv_done, CONV_OPS * i + CONV_OPS // 2 * (b + 1))
                    nc.scalar.activation(chunks(i, half_tanh)[:, 2 * b:2 * b + 2, :], chunks(i, conv)[:, 2 * b:2 * b + 2, :], ACT.Tanh,
                                         scale=0.5).then_inc(conv_tanh, 1)

            def softplus_exp(i):
                act.wait_ge(dt_done, i + 1)
                for c in range(KI):
                    nc.scalar.activation(chunks(i, soft)[:, c, :], BC[0][:, 0:width(i)], ACT.Abs, scale=dt_scale[:, c:c + 1],
                                         bias=dt_bias[:, c:c + 1])
                    last = nc.scalar.activation(chunks(i, delta)[:, c, :], BC[0][:, 0:width(i)], ACT.Relu, scale=dt_scale[:, c:c + 1],
                                                bias=dt_bias[:, c:c + 1])
                last.then_inc(soft_step, 1)
                act.wait_ge(soft_step, 3 * i + 1)
                nc.scalar.activation(chunks(i, soft), chunks(i, soft), ACT.Exp, scale=-1.0).then_inc(soft_step, 1)

            def softplus_ln(i):
                act.wait_ge(small_done, i + 1)
                nc.scalar.activation(chunks(i, series), chunks(i, small), ACT.Identity, scale=-0.5, bias=one_col[:]).then_inc(series_done, 1)
                nc.scalar.activation(chunks(i, soft), chunks(i, soft), ACT.Ln, bias=one_col[:]).then_inc(soft_step, 1)

            def decays(i, p, k):
                s, k = SCANS * p + k, k % SCANS
                act.wait_ge(decay_free, STATES * i + s + 1)
                for c in range(KI):
                    last = nc.scalar.activation(
                        decay[k][:, c * width(i):(c + 1) * width(i)].rearrange("p (a t) -> p a t", t=TOKENS)[:, :, 1:TOKENS],
                        chunks(i, delta)[:, c, :].rearrange("p (a t) -> p a t", a=images(i))[:, :, 1:TOKENS],
                        ACT.Exp, scale=aneg[:, s, c:c + 1])
                last.then_inc(decay_done, 1)

            def copy_bc(i, p, k):
                s, q, k = SCANS * p + k, k % 2, k % SCANS
                act.wait_ge(bc_done, STATES * i + s + 1)
                act.wait_ge(y_added, STATES * i + s + 1)
                nc.scalar.activation(chunks(i, spread_bc[k]), two(i, BC[q]), ACT.Copy).then_inc(bc_copied, 1)

            def start_y(i):
                act.wait_ge(mixer_setup, 1)
                act.wait_ge(x2_done, 2 * i + 2)
                for c in range(KI):
                    last = nc.scalar.activation(chunks(i, y)[:, c, :], chunks(i, x2)[:, c, :], ACT.Copy,
                                                scale=half_d[:, c:c + 1])
                last.then_inc(y_init, 1)

            def gate_tanh(t, p, k):
                for j in range(2):
                    act.wait_ge(gu_done, 2 * pair_index(t, p, k) + j + 1)
                    nc.scalar.activation(chunks(t, tanh_g)[:, j, :], GU[j][:, 0:width(t)], ACT.Tanh, scale=0.5).then_inc(tanh_done, 1)

            def copy_weights(t, p, k):
                act.wait_ge(wb_done, pair_index(t, p, k) + 1)
                act.wait_ge(weighted, set_credit(t, p, k))
                nc.scalar.activation(chunks(t, spread_w[k]), two(t, W), ACT.Copy).then_inc(wb_free, 1)

            def pair(t, p, k):
                gate_tanh(t, p, k)
                copy_weights(t, p, k)

            def square(no, sems):
                act.wait_ge(sems["centred"], no + 1)
                nc.scalar.activation(chunks(no, squared), chunks(no, centred), ACT.Square).then_inc(sems["squared"], 1)

            def read_variance(no, sems, bank):
                act.wait_ge(sems["var"], no + 1)
                nc.scalar.activation(var_eps[:, 0:width(no)], bank[:, 0:width(no)], ACT.Identity, bias=eps_col[:]).then_inc(sems["eps"], 1)

            def rough_rstd(no, sems):
                act.wait_ge(sems["eps"], no + 1)
                nc.scalar.activation(rough[:, 0:width(no)], var_eps[:, 0:width(no)], ACT.Ln).then_inc(sems["rough"], 1)
                act.wait_ge(sems["rough"], 2 * no + 1)
                nc.scalar.activation(rough[:, 0:width(no)], rough[:, 0:width(no)], ACT.Exp, scale=-0.5).then_inc(sems["rough"], 1)

            def scans(i, mixer, experts):
                def one_round(p, final):
                    for k in range(SETS):
                        if experts:
                            pair(i - 1, p, k)
                        for ahead in AHEAD_DECAY[k]:
                            if mixer and not (final and ahead >= SCANS):
                                decays(i, p, ahead)
                        for ahead in AHEAD_BC[k]:
                            if mixer and not (final and ahead >= SCANS):
                                copy_bc(i, p, ahead)

                with act.Fori(0, ROUNDS - 1) as p:
                    one_round(p, False)
                if mixer:
                    tanh_z(i)
                one_round(ROUNDS - 1, True)

            def turn(i, end, old, nxt):
                t, n = i - 1, i + 1
                if old:
                    pair(t, *LAST_BUT_ONE)
                if end:
                    square(i, mix_norm)
                    nc.scalar.preload_act_table_set("natural_log_exp_and_others")
                    read_variance(i, mix_norm, W)
                    rough_rstd(i, mix_norm)
                if old:
                    pair(t, *LAST)
                if nxt:
                    read_x(n)
                if end:
                    act.wait_ge(logits_done, i + 1)
                    nc.scalar.activation(ex[0:half(i)], W[0:half(i), 0:2 * EXPERTS].rearrange("p (b e) -> p b e", b=2), ACT.Exp,
                                         scale=-1.0).then_inc(ex_done, 1)
                if nxt:
                    tanh_conv(n)
                if end:
                    act.wait_ge(shared_gu, i + 1)
                    nc.scalar.activation(tanh_s[:, 0:width(i)], GU[0][:, 0:width(i)], ACT.Tanh, scale=0.5).then_inc(shared_tanh, 1)
                if old:
                    square(t, out_norm)
                if end:
                    nc.scalar.activation(chunks(i, h1_kept), chunks(i, h1), ACT.Copy).then_inc(h1_kept_done, 1)
                if nxt:
                    start_y(n)
                    softplus_exp(n)
                if old:
                    read_variance(t, out_norm, O)
                if end:
                    gate_tanh(i, *FIRST)
                nc.scalar.preload_act_table_set("natural_log_exp_and_others")
                if nxt:
                    softplus_ln(n)
                if old:
                    rough_rstd(t, out_norm)
                if end:
                    gate_tanh(i, *SECOND)
                    copy_weights(i, *FIRST)
                if nxt:
                    for k in range(SCANS - 1):
                        copy_bc(n, 0, k)
                    act.wait_ge(delta_done, n + 1)
                    decays(n, 0, 0)
                    decays(n, 0, 1)
                if end:
                    copy_weights(i, *SECOND)

            periods(act, scans, turn)

        @block.vector
        def _(dve):
            dve.sem_inc(decay_free, SCANS)
            dve.sem_inc(gu_free, 2)
            dve.sem_inc(wb_free, 1)
            dve.sem_inc(weighted, SETS)

            nc.vector.memset(one_col[:], 1.0)
            nc.vector.memset(eps_col[:], EPS)
            nc.vector.memset(small_col[:], SMALL)
            nc.vector.memset(averager[:], 1.0 / DM).then_inc(columns_done, 1)
            dve.wait_ge(embed_in, 16 * len(EMBED_LOADS))
            for m in range(KM):
                nc.vector.tensor_scalar(posb[:, m, 0:1], posb[:, m, 0:1], clsb[:, m:m + 1], None, ALU.add)
                last = nc.vector.tensor_scalar(posb[:, m, 1:TOKENS], posb[:, m, 1:TOKENS], tokb[:, m:m + 1], None, ALU.add)
            last.then_inc(posb_step, 1)
            dve.wait_ge(posb_step, 1)
            dve.wait_ge(cleared, CLEARED)

            def set_up_mixer():
                dve.wait_ge(mixer_in, 16 * len(MIXER_LOADS))
                for part in range(3):
                    nc.vector.tensor_scalar(xw[:, :, part, :], xw_raw[:, :, 1:1 + ROWS], 0.5, None, ALU.mult)
                nc.vector.tensor_scalar(dtw[:], xw_raw[:, :, 0:1].broadcast_to([P, KI, P]), 0.5, None, ALU.mult)
                dve.wait_ge(aexp_done, 2)
                nc.vector.tensor_scalar(aneg[:].rearrange("p s c -> p c s"), aexp[:].rearrange("p (c s) -> p c s", c=KI),
                                        -1.0, None, ALU.mult)
                nc.vector.tensor_scalar(half_d[:], dpar[:], 0.5, None, ALU.mult).then_inc(mixer_setup, 1)

            def split(no, step, bank, rows):
                base = SPLITS * no
                nc.vector.tensor_copy(rows[:, 0:width(no)], bank[0:SPLIT, 0:width(no)]).then_inc(step, 1)
                dve.wait_ge(step, base + 1)
                nc.vector.tensor_tensor(rest[:, 0:width(no)], bank[0:SPLIT, 0:width(no)], rows[:, 0:width(no)], ALU.subtract).then_inc(step, 1)
                dve.wait_ge(step, base + 2)
                nc.vector.tensor_copy(mid[:, 0:width(no)], rest[:, 0:width(no)]).then_inc(step, 1)
                dve.wait_ge(step, base + 3)
                nc.vector.tensor_copy(rows[ROWS:2 * ROWS, 0:width(no)], mid[ROWS:2 * ROWS, 0:width(no)])
                nc.vector.tensor_tensor(rows[2 * ROWS:SPLIT, 0:width(no)], rest[2 * ROWS:SPLIT, 0:width(no)], mid[2 * ROWS:SPLIT, 0:width(no)],
                                        ALU.subtract).then_inc(step, 1)

            def tokens(i):
                dve.wait_ge(tok_done, i + 1)
                for m in range(KM):
                    h0m = chunks(i, h0)[:, m, :].rearrange("p (a t) -> p a t", a=images(i))
                    nc.vector.tensor_tensor(
                        h0m[:, :, 1:TOKENS], BC[0][:, m * PATCHES * images(i):(m + 1) * PATCHES * images(i)].rearrange("p (a t) -> p a t", a=images(i)),
                        posb[:, m:m + 1, 1:TOKENS].broadcast_to([P, images(i), PATCHES]), ALU.add)
                    last = nc.vector.tensor_copy(h0m[:, :, 0:1], posb[:, m:m + 1, 0:1].broadcast_to([P, images(i), 1]))
                last.then_inc(h0_done, 1)

            def convolve(i, b):
                for k in range(TAPS - 1):
                    for c in range(2 * b, 2 * b + 2):
                        if k == 0:
                            dve.wait_ge(xpad_done, KI * i + c + 1)
                            dve.wait_ge(tap_done, KI * i + c + 1)
                        else:
                            dve.wait_ge(conv_done, CONV_OPS * i + CONV_OPS // 2 * b + 2 * (k - 1) + c % 2 + 1)
                        convc = chunks(i, conv)[:, c, :].rearrange("p (a t) -> p a t", a=images(i))
                        nc.vector.scalar_tensor_tensor(convc, xpad[:, c, 0:images(i), k:k + TOKENS], convw[:, c, k:k + 1],
                                                       convc, ALU.mult, ALU.add).then_inc(conv_done, 1)

            def silu_z(i):
                for b in range(2):
                    dve.wait_ge(z_tanh, 2 * i + b + 1)
                    nc.vector.scalar_tensor_tensor(chunks(i, z2)[:, 2 * b:2 * b + 2, :], chunks(i, half_tanh_z)[:, 2 * b:2 * b + 2, :], 1.0,
                                                   two(i, Z_BANKS[b]), ALU.add, ALU.mult).then_inc(z2_done, 1)

            def silu_conv(i):
                for b in range(2):
                    dve.wait_ge(conv_tanh, 2 * i + b + 1)
                    nc.vector.scalar_tensor_tensor(chunks(i, x2)[:, 2 * b:2 * b + 2, :], chunks(i, half_tanh)[:, 2 * b:2 * b + 2, :], 1.0,
                                                   chunks(i, conv)[:, 2 * b:2 * b + 2, :], ALU.add, ALU.mult).then_inc(x2_done, 1)

            def softplus_small(i):
                dve.wait_ge(soft_step, 3 * i + 2)
                nc.vector.tensor_scalar(chunks(i, small), chunks(i, soft), SMALL, None, ALU.min).then_inc(small_done, 1)

            def softplus_sum(i):
                dve.wait_ge(soft_step, 3 * i + 3)
                nc.vector.scalar_tensor_tensor(chunks(i, soft), chunks(i, soft), ln_small[:], chunks(i, delta), ALU.max,
                                               ALU.add).then_inc(softplus_step, 1)
                dve.wait_ge(softplus_step, i + 1)
                dve.wait_ge(product_done, i + 1)
                nc.vector.scalar_tensor_tensor(chunks(i, delta), chunks(i, soft), ln_small[:], chunks(i, small), ALU.subtract,
                                               ALU.add).then_inc(delta_done, 1)

            def delta_x(i):
                dve.wait_ge(delta_done, i + 1)
                nc.vector.scalar_tensor_tensor(chunks(i, du), chunks(i, x2), 0.5, chunks(i, delta), ALU.mult, ALU.mult).then_inc(du_done, 1)
                dve.wait_ge(du_done, i + 1)

            def shared_expert(t):
                dve.wait_ge(shared_tanh, t + 1)
                nc.vector.scalar_tensor_tensor(act_s[:, 0:width(t)], tanh_s[:, 0:width(t)], 1.0, GU[0][:, 0:width(t)], ALU.add,
                                               ALU.mult).then_inc(shared_step, 1)
                dve.wait_ge(shared_step, 2 * t + 1)
                nc.vector.scalar_tensor_tensor(hid_s[:, 0:width(t)], act_s[:, 0:width(t)], 0.5, GU[1][:, 0:width(t)], ALU.mult,
                                               ALU.mult).then_inc(shared_step, 1)

            def drives(i, p, k):
                s, q, k = SCANS * p + k, k % 2, k % SCANS
                dve.wait_ge(bc_copied, STATES * i + s + 3)
                nc.vector.tensor_tensor(chunks(i, drive[q]), chunks(i, du),
                                        spread_bc[k][:, None, 0:width(i)].broadcast_to([P, KI, width(i)]),
                                        ALU.mult).then_inc(drive_done, 1)

            def scan(i, p, k):
                s, q, k = SCANS * p + k, k % 2, k % SCANS
                dve.wait_ge(decay_done, STATES * i + s + 1)
                dve.wait_ge(drive_done, STATES * i + s + 1)
                dve.wait_ge(y_added, STATES * i + s + 1)
                nc.vector.tensor_tensor_scan(state[k][:, 0:KI * width(i)], decay[k][:, 0:KI * width(i)],
                                             drive[q][:, 0:KI * width(i)], 0.0, ALU.mult, ALU.add).then_inc(decay_free, 1)

            def reads(i, p, k):
                dve.wait_ge(decay_free, STATES * i + SCANS * p + k + 1 + SCANS)
                nc.vector.tensor_tensor(
                    chunks(i, read[k]), chunks(i, state[k]),
                    spread_bc[k][:, None, width(i):2 * width(i)].broadcast_to([P, KI, width(i)]),
                    ALU.mult).then_inc(read_done, 1)

            def act_gate(t, p, k, j):
                dve.wait_ge(tanh_done, 2 * pair_index(t, p, k) + j + 1)
                nc.vector.scalar_tensor_tensor(chunks(t, act_g)[:, j, :], chunks(t, tanh_g)[:, j, :], 1.0, GU[j][:, 0:width(t)], ALU.add,
                                               ALU.mult).then_inc(act_done, 1)

            def times_up(t, p, k, j):
                dve.wait_ge(act_done, 2 * pair_index(t, p, k) + j + 1)
                if j == 0:
                    dve.wait_ge(weighted, set_credit(t, p, k))
                nc.vector.tensor_tensor(chunks(t, hid[k])[:, j, :], chunks(t, act_g)[:, j, :], GU[j][:, width(t):2 * width(t)], ALU.mult).then_inc(gu_free, 1)

            def hidden(t, p, k):
                for j in range(2):
                    act_gate(t, p, k, j)
                    times_up(t, p, k, j)

            def centre(no, sems, source, bank):
                dve.wait_ge(sems["mean"], no + 1)
                nc.vector.tensor_tensor(chunks(no, centred), chunks(no, source), bank[:, None, 0:width(no)].broadcast_to([P, KM, width(no)]),
                                        ALU.subtract).then_inc(sems["centred"], 1)

            def router(i):
                done = [0]

                def in_turn(ins):
                    done[0] += 1
                    ins.then_inc(route_step, 1)
                    dve.wait_ge(route_step, ROUTE * i + done[0])

                def gate():
                    dve.sem_inc(route_gate, 1)

                dve.wait_ge(ex_done, i + 1)
                in_turn(nc.vector.tensor_scalar(ex[0:half(i)], ex[0:half(i)], 1.0, None, ALU.add))
                in_turn(nc.vector.reciprocal(score[0:half(i)], ex[0:half(i)]))
                in_turn(nc.vector.tensor_reduce(gsum[0:half(i), :, 0:GROUPS],
                                                score[0:half(i)].rearrange("p b (g e) -> p b g e", g=GROUPS), AX.X, ALU.add))
                for b in range(2):
                    gate()
                    in_turn(nc.vector.max(gtop[0:half(i), b, :], gsum[0:half(i), b, :]))
                in_turn(nc.vector.tensor_copy(glist[0:half(i), :, 0:TOPG], gtop[0:half(i), :, 0:TOPG]))
                for b in range(2):
                    gate()
                    in_turn(nc.vector.match_replace(gleft[0:half(i), b, :], glist[0:half(i), b, :], gsum[0:half(i), b, :], -1.0))
                in_turn(nc.vector.tensor_scalar(gmask[0:half(i)], gleft[0:half(i), :, 0:GROUPS], -1.0, None, ALU.is_equal))
                in_turn(nc.vector.tensor_tensor(
                    masked[0:half(i)].rearrange("p b (g e) -> p b g e", g=GROUPS), score[0:half(i)].rearrange("p b (g e) -> p b g e", g=GROUPS),
                    gmask[0:half(i), :, :, None].broadcast_to([half(i), 2, GROUPS, PER_GROUP]), ALU.mult))
                for b in range(2):
                    gate()
                    in_turn(nc.vector.max(etop[0:half(i), b, :], masked[0:half(i), b, :]))
                for b in range(2):
                    gate()
                    in_turn(nc.vector.match_replace(eleft[0:half(i), b, :], etop[0:half(i), b, :], masked[0:half(i), b, :], -1.0))
                in_turn(nc.vector.scalar_tensor_tensor(wsel[0:half(i)], eleft[0:half(i)], -1.0, masked[0:half(i)], ALU.is_equal, ALU.mult))
                in_turn(nc.vector.tensor_reduce(wsum[0:half(i)], wsel[0:half(i)], AX.X, ALU.add))
                in_turn(nc.vector.tensor_scalar(wsum[0:half(i)], wsum[0:half(i)], 1e-12, None, ALU.max))
                in_turn(nc.vector.reciprocal(winv[0:half(i)], wsum[0:half(i)]))
                for b in range(2):
                    last = nc.vector.tensor_scalar(w3[0:half(i), b], wsel[0:half(i), b:b + 1, :].broadcast_to([half(i), 3, EXPERTS]),
                                                   winv[0:half(i), b:b + 1], 0.5, ALU.mult, ALU.mult)
                last.then_inc(route_step, 1)
                assert done[0] + 1 == ROUTE, done

            def scans(i, mixer, experts):
                t = i - 1

                def one_round(p, final):
                    for k in range(SETS):
                        if experts:
                            act_gate(t, p, k, 0)
                        if mixer:
                            if k == 1:
                                scan(i, p, 2)
                            else:
                                reads(i, p, (0, None, 3)[k])
                        if experts:
                            times_up(t, p, k, 0)
                            act_gate(t, p, k, 1)
                        if mixer and not (final and k == 2):
                            drives(i, p, (1, 3, 4)[k])
                        if experts:
                            times_up(t, p, k, 1)
                        if mixer:
                            if k == 0:
                                scan(i, p, 1)
                                drives(i, p, 2)
                            elif k == 1:
                                reads(i, p, 2)
                                scan(i, p, 3)
                            elif not final:
                                scan(i, p, 4)

                with dve.Fori(0, ROUNDS - 1) as p:
                    one_round(p, False)
                one_round(ROUNDS - 1, True)

            def turn(i, end, old, nxt):
                t, n = i - 1, i + 1
                if end:
                    silu_z(i)
                if old:
                    hidden(t, *LAST_BUT_ONE)
                if end:
                    dve.wait_ge(z2_done, 2 * i + 2)
                    dve.wait_ge(y_added, STATES * (i + 1) + SCANS)
                    for b in range(2):
                        nc.vector.scalar_tensor_tensor(chunks(i, gated)[:, 2 * b:2 * b + 2, :], chunks(i, y)[:, 2 * b:2 * b + 2, :],
                                                       0.5, chunks(i, z2)[:, 2 * b:2 * b + 2, :], ALU.mult,
                                                       ALU.mult).then_inc(gated_done, 1)
                    dve.wait_ge(outproj_done, i + 1)
                    nc.vector.tensor_tensor(chunks(i, r1), two(i, Y[0]), chunks(i, h0), ALU.add).then_inc(mix_norm["sum"], 1)
                    centre(i, mix_norm, r1, W)
                if nxt:
                    tokens(n)
                    if not end:
                        set_up_mixer()
                if end:
                    normalise(dve, nc.vector, i, mix_norm, h1)
                if old:
                    hidden(t, *LAST)
                if nxt:
                    convolve(n, 0)
                if old:
                    dve.wait_ge(hidw_free, PAIRS * (t + 1) + SETS)
                    dve.wait_ge(h1_kept_done, t + 1)
                    nc.vector.tensor_tensor(chunks(t, r2), two(t, O), chunks(t, h1_kept), ALU.add).then_inc(out_norm["sum"], 1)
                if nxt:
                    convolve(n, 1)
                    silu_conv(n)
                if old:
                    dve.wait_ge(out_norm["sum"], t + 1)
                    centre(t, out_norm, r2, O)
                if end:
                    shared_expert(i)
                    router(i)
                if nxt:
                    dve.wait_ge(rows_done, n + 1)
                    split(n, bc_split, BC[1], bc_rows)
                    softplus_small(n)
                if end:
                    hidden(i, *FIRST)
                    dve.wait_ge(w3_turned, i + 1)
                    split(i, w_split, W, w_rows)
                if nxt:
                    softplus_sum(n)
                if end:
                    hidden(i, *SECOND)
                if nxt:
                    delta_x(n)
                    drives(n, 0, 0)
                    scan(n, 0, 0)
                if old and not end:
                    dve.wait_ge(out_sent, 16 * (t + 1))
                    normalise(dve, nc.vector, t, out_norm, outb)

            periods(dve, scans, turn)


def kernel(**inputs):
    import numpy as _np
    import concourse.bacc as _bacc
    from concourse import mybir as _mybir
    from concourse.bass_utils import run_bass_kernel_spmd as _run

    a = {k: _np.asarray(v) for k, v in inputs.items()}

    def rows(w):
        w = w.reshape(w.shape[0] // P, P, *w.shape[1:])
        return w.transpose(1, 0, *range(2, w.ndim))

    x = _np.zeros((TILES * TI, CHANNELS, GRID, PATCH, GRID, PATCH), a["x"].dtype)
    rows_of = _np.r_[0:FIRST_IMAGES, TI:TILES * TI]
    x[rows_of] = a["x"].reshape(IMAGES, CHANNELS, GRID, PATCH, GRID, PATCH)
    x = x.reshape(TILES, TI, CHANNELS, GRID, PATCH, GRID, PATCH).transpose(0, 2, 4, 6, 1, 3, 5)
    x = x.reshape(TILES, KF, P, NP).transpose(0, 2, 1, 3)

    def expert(gate, up, down):
        e = gate.shape[0]
        g, u = (w.transpose(0, 2, 1).reshape(e, KM, P, HID).transpose(0, 2, 1, 3).reshape(e, P, KM * HID)
                for w in (gate, up))
        return _np.concatenate([g, u, down.transpose(0, 2, 1)], axis=2)

    experts = expert(a["L0_ffn_expert_gate"], a["L0_ffn_expert_up"], a["L0_ffn_expert_down"])
    experts = experts.reshape(PAIRS, 2, P, WCOLS).transpose(0, 2, 1, 3)

    given = {
        "x": x,
        "w_tok": rows(a["L0_tok_W"].T),
        "b_tok": rows(a["L0_tok_b"]),
        "cls_tok": rows(a["L0_tok_cls_token"].reshape(DM)),
        "pos": rows(a["L0_tok_pos_enc"][0].T),
        "w_in": rows(a["L0_attn_W_in"].T),
        "conv_w": rows(a["L0_attn_conv_w"][:, 0, :]),
        "conv_b": rows(a["L0_attn_conv_b"]),
        "w_x": rows(a["L0_attn_W_x"].T),
        "w_dt": rows(a["L0_attn_W_dt"][:, 0]),
        "b_dt": rows(a["L0_attn_b_dt"]),
        "a_log": rows(a["L0_attn_A_log"]).reshape(P, KI * STATES),
        "d_par": rows(a["L0_attn_D_param"]),
        "w_out": rows(a["L0_attn_W_out"].T),
        "gate_w": rows(a["L0_ffn_gate_w"].T),
        "experts": experts,
        "shared": expert(*(a[f"L0_ffn_shared_{n}_w"][None] for n in ("gate", "up", "down")))[0],
    }
    nc = _bacc.Bacc("TRN2", target_bir_lowering=False, num_devices=1)
    arrays, args = {}, []
    for name, v in given.items():
        v = _np.ascontiguousarray(v)
        arrays[f"in_{name}_dram"] = v
        args.append(nc.dram_tensor(f"in_{name}_dram", v.shape, _mybir.dt.from_np(v.dtype), kind="ExternalInput").ap())
    args.append(nc.dram_tensor("out_dram", (TILES, P, KM, N), _mybir.dt.float32, kind="ExternalOutput").ap())
    build(nc, *args)
    r = _run(nc, [arrays], core_ids=[0])
    got = r.results[0]["out_dram"].reshape(TILES, P, KM, TI, TOKENS).transpose(0, 3, 4, 2, 1)
    return _np.ascontiguousarray(got.reshape(TILES * TI, TOKENS, DM)[rows_of])
```
